# Optimizing a Trainium2 kernel written in Bass

```python
import numpy as np
import jax
import jax.numpy as jnp

def _softmax(x, axis=-1):
    return jax.nn.softmax(x, axis=axis)

def _gelu(x):
    return jax.nn.gelu(x, approximate=True)

def _silu(x):
    return jax.nn.silu(x)

def _sigmoid(x):
    return jax.nn.sigmoid(x)

def _layernorm(x, axis=-1, eps=1e-05):
    m = jnp.mean(x, axis=axis, keepdims=True)
    v = jnp.var(x, axis=axis, keepdims=True)
    return (x - m) / jnp.sqrt(v + eps)

def _scatter_add(tgt, idx, src, axis=0):
    return tgt.at[idx].add(src)

def _segment_sum(src, seg, n):
    return jax.ops.segment_sum(src, seg, n)
kernel_name = 'mk_xattn_ffn_d1_seqx_r4_cf1e5e'

def setup_inputs(seed: int=0):
    np.random.seed(seed)
    _w = jnp.asarray

    def _rec_inputs():
        import jax
        import jax.numpy as jnp
        _rk = jax.random.key(seed)
        x = -0.0002928 + 1 * jax.random.normal(jax.random.fold_in(_rk, 1), (16, 512, 256), jnp.float32)
        _lenS = 512 - jax.random.randint(jax.random.fold_in(_rk, 7), (16,), 0, max(1, 512 // 4) + 1, jnp.int32)
        _lenS2 = 64 - jax.random.randint(jax.random.fold_in(_rk, 8), (16,), 0, max(1, 64 // 4) + 1, jnp.int32)
        _ctx_1024P = jax.random.normal(jax.random.fold_in(_rk, 11), (16, 16, 256), jnp.float32)
        _ctx_1024c = jax.random.dirichlet(jax.random.fold_in(_rk, 511), 0.3 * jnp.ones((16,), jnp.float32), (16, 64))
        _ctx_1024t = jnp.einsum('bsk,bkd->bsd', _ctx_1024c, _ctx_1024P)
        _ctx_1024t = _ctx_1024t * jax.lax.rsqrt(jnp.mean(jnp.square(_ctx_1024t)) + 1e-12) * 0.953939
        ctx_1024 = -1.39393e-06 + 0.999914 * (_ctx_1024t + 0.3 * jax.random.normal(jax.random.fold_in(_rk, 611), (16, 64, 256), jnp.float32))
        return (x, ctx_1024)
    x, ctx_1024 = _rec_inputs()

    def _L0_xattn_setup():
        import jax, jax.numpy as jnp
        import numpy as np
        B, N, D_MODEL, H, DH = (2, 512, 256, 16, 64)
        SCALE = DH ** (-0.5)
        key = jax.random.key(seed)
        ks = jax.random.split(key, 6)

        def lin(k, fan_in, shape):
            return jax.random.normal(k, shape, dtype=jnp.float32) / np.sqrt(fan_in)
        return {'x': jax.random.normal(ks[0], (B, N, D_MODEL), dtype=jnp.float32), 'context': jax.random.normal(ks[1], (B, N, D_MODEL), dtype=jnp.float32), 'Wq': lin(ks[2], D_MODEL, (D_MODEL, H * DH)), 'Wk': lin(ks[3], D_MODEL, (D_MODEL, H * DH)), 'Wv': lin(ks[4], D_MODEL, (D_MODEL, H * DH)), 'Wo': lin(ks[5], H * DH, (H * DH, D_MODEL)), 'bo': jnp.zeros((D_MODEL,), dtype=jnp.float32)}
    _L0_xattn_all = _L0_xattn_setup()
    _L0_xattn_in = {k: v for k, v in _L0_xattn_all.items() if k in ('Wq', 'Wk', 'Wv', 'Wo', 'bo')}
    del _L0_xattn_all

    def _L0_ffn_setup():
        import jax, jax.numpy as jnp
        import numpy as np
        from jax import lax
        DIM = 256
        INTER = 128
        N_EXPERTS = 16
        TOPK = 4
        ROUTE_SCALE = 2.5
        VOCAB = 8000

        def _silu_and_mul(gu):
            gate, up = jnp.split(gu, 2, axis=-1)
            return jax.nn.silu(gate) * up
        key = jax.random.key(seed)
        ks = jax.random.split(key, 8)
        x = jax.random.normal(ks[0], (2, 128, DIM), dtype=jnp.float32)
        input_ids = jax.random.randint(ks[1], (2, 128), 0, VOCAB)
        s = 0.02
        gate_w = jax.random.normal(ks[2], (N_EXPERTS, DIM), dtype=jnp.float32) * s
        gate_b = jax.random.normal(ks[3], (N_EXPERTS,), dtype=jnp.float32) * s
        w13 = jax.random.normal(ks[4], (N_EXPERTS, 2 * INTER, DIM), dtype=jnp.float32) * s
        w2 = jax.random.normal(ks[5], (N_EXPERTS, DIM, INTER), dtype=jnp.float32) * s
        w13_s = jax.random.normal(ks[6], (2 * INTER, DIM), dtype=jnp.float32) * s
        w2_s = jax.random.normal(ks[7], (DIM, INTER), dtype=jnp.float32) * s
        return {'x': x, 'input_ids': input_ids, 'gate_w': gate_w, 'gate_b': gate_b, 'w13': w13, 'w2': w2, 'w13_s': w13_s, 'w2_s': w2_s}
    _L0_ffn_all = _L0_ffn_setup()
    _L0_ffn_in = {k: v for k, v in _L0_ffn_all.items() if k in ('input_ids', 'gate_w', 'gate_b', 'w13', 'w2', 'w13_s', 'w2_s')}
    del _L0_ffn_all
    return {'x': x, 'ctx_1024': ctx_1024, 'L0_xattn_Wq': _L0_xattn_in['Wq'], 'L0_xattn_Wk': _L0_xattn_in['Wk'], 'L0_xattn_Wv': _L0_xattn_in['Wv'], 'L0_xattn_Wo': _L0_xattn_in['Wo'], 'L0_xattn_bo': _L0_xattn_in['bo'], 'L0_ffn_input_ids': _L0_ffn_in['input_ids'], 'L0_ffn_gate_w': _L0_ffn_in['gate_w'], 'L0_ffn_gate_b': _L0_ffn_in['gate_b'], 'L0_ffn_w13': _L0_ffn_in['w13'], 'L0_ffn_w2': _L0_ffn_in['w2'], 'L0_ffn_w13_s': _L0_ffn_in['w13_s'], 'L0_ffn_w2_s': _L0_ffn_in['w2_s']}

def reference(x, ctx_1024, L0_xattn_Wq, L0_xattn_Wk, L0_xattn_Wv, L0_xattn_Wo, L0_xattn_bo, L0_ffn_input_ids, L0_ffn_gate_w, L0_ffn_gate_b, L0_ffn_w13, L0_ffn_w2, L0_ffn_w13_s, L0_ffn_w2_s):
    import jax
    import jax.numpy as jnp

    def _L0_xattn_ref(x, context, Wq, Wk, Wv, Wo, bo):
        import jax, jax.numpy as jnp
        import numpy as np
        B, N, D_MODEL, H, DH = (2, 512, 256, 16, 64)
        SCALE = DH ** (-0.5)
        b, n, _ = x.shape
        m = context.shape[1]
        q = (x @ Wq).reshape(b, n, H, DH)
        k = (context @ Wk * SCALE).reshape(b, m, H, DH)
        v = (context @ Wv).reshape(b, m, H, DH)
        scores = jnp.einsum('bihd,bjhd->bhij', q, k)
        attn = jax.nn.softmax(scores, axis=-1)
        out = jnp.einsum('bhij,bjhd->bihd', attn, v)
        out = out.reshape(b, n, H * DH)
        return out @ Wo + bo

    def _L0_ffn_ref(x, input_ids, gate_w, gate_b, w13, w2, w13_s, w2_s):
        import jax, jax.numpy as jnp
        import numpy as np
        from jax import lax
        DIM = 256
        INTER = 128
        N_EXPERTS = 16
        TOPK = 4
        ROUTE_SCALE = 2.5
        VOCAB = 8000

        def _silu_and_mul(gu):
            gate, up = jnp.split(gu, 2, axis=-1)
            return jax.nn.silu(gate) * up
        B, S, D = x.shape
        xt = x.reshape(-1, D)
        T = xt.shape[0]
        scores = jax.nn.sigmoid(xt.astype(jnp.float32) @ gate_w.T)
        biased = scores + gate_b
        _, idx = lax.top_k(biased, TOPK)
        w = jnp.take_along_axis(scores, idx, axis=-1)
        w = w / jnp.sum(w, axis=-1, keepdims=True)
        w = w * ROUTE_SCALE
        comb = jnp.zeros((T, N_EXPERTS), jnp.float32)
        comb = comb.at[jnp.arange(T)[:, None], idx].add(w)
        comb = comb.astype(x.dtype)

        def expert_body(y, args):
            w13_e, w2_e, c_e = args
            h = _silu_and_mul(xt @ w13_e.T)
            return (y + c_e[:, None] * (h @ w2_e.T), None)
        y, _ = lax.scan(expert_body, jnp.zeros_like(xt), (w13, w2, comb.T))
        y = y + _silu_and_mul(xt @ w13_s.T) @ w2_s.T
        return y.astype(x.dtype).reshape(B, S, D)
    x = x + _L0_xattn_ref(_layernorm(x, axis=-1), ctx_1024, L0_xattn_Wq, L0_xattn_Wk, L0_xattn_Wv, L0_xattn_Wo, L0_xattn_bo)
    x = x + _L0_ffn_ref(_layernorm(x, axis=-1), L0_ffn_input_ids, L0_ffn_gate_w, L0_ffn_gate_b, L0_ffn_w13, L0_ffn_w2, L0_ffn_w13_s, L0_ffn_w2_s)
    return x

_drawn_inputs = setup_inputs


def setup_inputs(seed=0):
    import zlib

    import numpy as np

    out = dict(_drawn_inputs(seed))
    spreads = {'L0_xattn_bo': (0.0, 0.1)}
    factors = {'L0_ffn_gate_w': 5.138,
     'L0_ffn_gate_b': 8.0,
     'L0_ffn_w13': 4.356,
     'L0_ffn_w2': 4.349,
     'L0_ffn_w13_s': 5.461,
     'L0_ffn_w2_s': 5.46}
    for name, (base, spread) in spreads.items():
        noise = np.random.default_rng([zlib.crc32(name.encode()), seed]).standard_normal(out[name].shape)
        drawn = base * np.exp(spread * noise) if base else spread * noise
        out[name] = jnp.asarray(drawn.astype(out[name].dtype))
    for name, factor in factors.items():
        out[name] = (out[name] * factor).astype(out[name].dtype)
    return out
```

```python
from contextlib import ExitStack

import concourse.bass as bass
from concourse import mybir

F32 = mybir.dt.float32
F32R = mybir.dt.float32r
ALU = mybir.AluOpType
ACT = mybir.ActivationFunctionType
AX = mybir.AxisListType

P = 128
B, N, D = 16, 512, 256
H, DH = 16, 64
C = 64
KD = D // P
PAIRS = H // 2
HC = H * C
TILES = B * N // P
TPB = N // P
E, I, TOPK = 16, 128, 4
EA = E + 1
SCALE = DH ** -0.5
ROUTE_SCALE = 2.5
EPS = 1e-5
BODY = 2 * TPB
TURNS = TILES // BODY
BASE_E = 2.718281828459045
NEVER = 3.0e38


def build(nc, x, ctxT, wq, wk, wv, wo, bo, gateT, gate_b, w13, w2, w13_s, w2_s, out):
    x_t = x.rearrange("b (t p) d -> (b t) p d", p=P)
    out_t = out.rearrange("b (t p) d -> (b t) p d", p=P)
    scratch = {
        "k": nc.dram_tensor("keys_scratch", [B, P, PAIRS, C], F32).ap(),
        "v": nc.dram_tensor("values_scratch", [B, P, PAIRS, C], F32).ap(),
        "x1": nc.dram_tensor("x1_scratch", [TILES, P, D], F32).ap(),
        "xn2T": nc.dram_tensor("xn2T_scratch", [TILES, P, KD, P], F32).ap(),
        "comb": nc.dram_tensor("comb_scratch", [TILES, P, E], F32).ap(),
    }
    with ExitStack() as outer:
        ident = outer.enter_context(nc.sbuf_tensor("ident", [P, P], F32))
        with ExitStack() as ctx:
            phase_a(nc, ctx, x_t, ctxT, wq, wk, wv, wo, bo, gateT, gate_b, ident, scratch)
        with ExitStack() as ctx:
            phase_b(nc, ctx, w13, w2, w13_s, w2_s, ident, scratch, out_t)


def turns(eng, body, count, drain, step):
    for u in range(body):
        step(0, u)
    with eng.Fori(1, count - 1) as i:
        for u in range(body):
            step(i, u)
    for u in range(body):
        step(count - 1, u)
    for u in range(drain):
        step(count, u)


QUARTER = [["T0", "T1", "U0"], ["G0", "G1", "U1"], ["G2", "G3", "U2"], ["U3"]]
PREP_ORDER = ["T0", "T1", "G0", "G1", "G2", "G3", "U0", "U1", "U2", "U3"]
OWN = [("RT", 2), ("O", 0), ("XT", 1)]


def side_jobs(m):
    prep = QUARTER[m % TPB] if m + TPB - m % TPB < TILES else []
    return list(prep) + [name for name, lag in OWN if 0 <= m - lag < TILES]


def jobs_before(m):
    return len(PREP_ORDER) + sum(len(side_jobs(w)) for w in range(m))


PER_TURN = jobs_before(3 * BODY) - jobs_before(2 * BODY)


class Job:

    def __init__(self, turn, at):
        self.count, self.before, self.bank = turn * PER_TURN + (at + 1), turn * (PER_TURN // 2) + at // 2, at % 2
        self.first = isinstance(turn, int) and turn == 0 and at < 2


def side_job(i, u, name):
    if isinstance(i, int):
        m = i * BODY + u
        return Job(0, jobs_before(m) + side_jobs(m).index(name))
    m = 2 * BODY + u
    return Job(i, jobs_before(m) + side_jobs(m).index(name) - 2 * PER_TURN)


def prep_job(i, u, name):
    if isinstance(i, int) and i * BODY + u < TPB:
        return Job(0, PREP_ORDER.index(name))
    quarter = [name in q for q in QUARTER].index(True)
    return side_job(i, u // TPB * TPB - TPB + quarter, name)


def valid(i, u, d):
    return 0 <= i * BODY + u + d < TILES if isinstance(i, int) else True


def prepares(i, u):
    return not isinstance(i, int) or i * BODY + u + TPB - u % TPB < TILES


def after_first(i, u):
    return not isinstance(i, int) or i * BODY + u >= 1


def phase_a(nc, ctx, x_t, ctxT, wq, wk, wv, wo, bo, gateT, gate_b, ident, scratch):
    k_d, v_d, x1_d, xn2T_d, comb_d = (scratch[k] for k in ("k", "v", "x1", "xn2T", "comb"))

    def sb(name, shape, dt=F32):
        return ctx.enter_context(nc.sbuf_tensor(name, shape, dt))

    def sem(name):
        return ctx.enter_context(nc.semaphore(name))

    bo_b = sb("bo_b", [P, D])
    gb_b = sb("gb_b", [P, TPB, E])
    gate = sb("gate", [P, KD, E])
    base_e = sb("base_e", [P, E])
    minus_half = sb("minus_half", [P, 2])
    eps = sb("eps", [P, 2])
    waited = sb("waited", [P, 2, 1])
    wqT = sb("wqT", [P, PAIRS, D])
    wo_s = sb("wo_s", [P, PAIRS, D])
    wk_s = sb("wk_s", [P, KD, H * DH])
    wv_s = sb("wv_s", [P, KD, H * DH])
    ctx_s = sb("ctx_s", [P, KD, B * C])
    kv_stage = sb("kv_stage", [P, 4, N])
    xin = sb("xin", [P, 4, D])
    xres = sb("xres", [P, 2, D])
    xn = sb("xn", [P, 2, TPB, D])
    xnT = sb("xnT", [P, 2, KD, N])
    keys = sb("keys", [P, 2, PAIRS, C])
    vbd = sb("vbd", [P, 2, PAIRS, P])
    G = sb("G", [P, 2, KD, HC])
    U = sb("U", [P, 2, PAIRS, D])
    probs = sb("probs", [P, 2, HC])
    probsT = sb("probsT", [P, 2, PAIRS, P])
    x1 = sb("x1", [P, 2, D])
    xn2 = sb("xn2", [P, 2, D])
    xn2T = sb("xn2T", [P, 2, KD, P])
    rowmax = sb("rowmax", [P, 2, H])
    rowsum = sb("rowsum", [P, 2, H])
    rowinv = sb("rowinv", [P, 2, H])
    bn = sb("bn", [P, 2, 2, 6])
    mv = sb("mv", [P, 2, 2, 2])
    veps = sb("veps", [P, 2, 2])
    rstd = sb("rstd", [P, 2, 2])
    neglog = sb("neglog", [P, 2, E])
    explog = sb("explog", [P, 2, TPB, E])
    denom = sb("denom", [P, TPB, E])
    score = sb("score", [P, TPB, E])
    biased = sb("biased", [P, TPB, E])
    top8 = sb("top8", [P, TPB, 8])
    rest = sb("rest", [P, TPB, E])
    picked = sb("picked", [P, TPB, E])
    weight = sb("weight", [P, TPB, E])
    wsum = sb("wsum", [P, TPB])
    winv = sb("winv", [P, TPB])
    comb = sb("comb", [P, 2, TPB, E])

    S = ctx.enter_context(nc.psum_tensor("S", [P, 2, HC], F32))
    PT = ctx.enter_context(nc.psum_tensor("PT", [P, PAIRS, P], F32))
    side = ctx.enter_context(nc.psum_tensor("side", [P, 2, N], F32))

    consts_in = sem("consts_in")
    wkv_in = sem("wkv_in")
    proj_full = sem("proj_full")
    proj_read = sem("proj_read")
    kv_stored = [sem(f"kv_stored{i}") for i in range(4)]
    xin_in = [sem(f"xin_in{i}") for i in range(4)]
    xres_in = [sem(f"xres_in{i}") for i in range(2)]
    kv_in = [sem(f"kv_in{i}") for i in range(2)]
    x1_stored = [sem(f"x1_stored{i}") for i in range(2)]
    xn2T_stored = [sem(f"xn2T_stored{i}") for i in range(2)]
    comb_stored = [sem(f"comb_stored{i}") for i in range(2)]
    ident_zero = sem("ident_zero")
    vbd_zero = sem("vbd_zero")
    consts_set = sem("consts_set")
    bn_done = sem("bn_done")
    stats_ready = sem("stats_ready")
    veps_ready = sem("veps_ready")
    rstd_ready = sem("rstd_ready")
    xn_ready = sem("xn_ready")
    xn2_ready = sem("xn2_ready")
    S_full = sem("S_full")
    max_ready = sem("max_ready")
    shifted = sem("shifted")
    exp_done = sem("exp_done")
    sum_ready = sem("sum_ready")
    inv_ready = sem("inv_ready")
    probs_ready = sem("probs_ready")
    residual_ready = sem("residual_ready")
    scored = sem("scored")
    biased_ready = sem("biased_ready")
    top_ready = sem("top_ready")
    picked_ready = sem("picked_ready")
    weight_ready = sem("weight_ready")
    wsum_ready = sem("wsum_ready")
    PT_full = sem("PT_full")
    probsT_ready = sem("probsT_ready")
    side_full = sem("side_full")
    side_read = [sem("side_read0"), sem("side_read1")]
    explog_ready = sem("explog_ready")
    comb_ready = sem("comb_ready")
    CONSTS = 16 * (4 + TPB)

    block = ctx.enter_context(nc.Block())

    def unloaded(eng, job):
        eng.wait_ge(side_read[job.bank], job.before + 1)

    def bank_free(eng, job):
        if not job.first:
            eng.wait_ge(side_read[job.bank], job.before)

    @block.sync
    def _(sp):
        for to, of in (wk_s, wk), (wv_s, wv):
            sp.dma_start(to[:], of.rearrange("(k p) n -> p k n", p=P)).then_inc(wkv_in, 16)
        sp.dma_start(ctx_s[:], ctxT.rearrange("(k p) n -> p k n", p=P)).then_inc(wkv_in, 16)
        for m in range(4):
            sp.dma_start(xin[:, m], x_t[m]).then_inc(xin_in[m], 16)
        sp.dma_start(wqT[:], wq.rearrange("(h p) n -> p h n", p=P)).then_inc(consts_in, 16)
        sp.dma_start(wo_s[:], wo.rearrange("(h p) n -> p h n", p=P)).then_inc(consts_in, 16)
        sp.dma_start(gate[:], gateT.rearrange("(k p) n -> p k n", p=P)).then_inc(consts_in, 16)
        sp.dma_start(bo_b[:], bo.rearrange("(a d) -> a d", a=1).to_broadcast([P, D])).then_inc(consts_in, 16)
        for t in range(TPB):
            sp.dma_start(gb_b[:, t], gate_b.rearrange("(a d) -> a d", a=1).to_broadcast([P, E])).then_inc(consts_in, 16)
        for m in range(4, 8):
            sp.wait_ge(xn_ready, m - 3)
            sp.dma_start(xin[:, m % 4], x_t[m]).then_inc(xin_in[m % 4], 16)
        for j in range(4 * PAIRS):
            to, pair, half = (k_d, v_d)[j // (2 * PAIRS)], j // 2 % PAIRS, j % 2
            sp.wait_ge(proj_read, j + 1)
            sp.dma_start(to[half * 8:half * 8 + 8, :, pair, :].rearrange("b p c -> p b c"),
                         kv_stage[:, j % 4].rearrange("p (b c) -> p b c", c=C)).then_inc(kv_stored[j % 4], 16)
        for s in range(4):
            sp.wait_ge(kv_stored[s], 16 * PAIRS)

        def load_kv(b, s):
            sp.dma_start(keys[:, s], k_d[b]).then_inc(kv_in[s], 16)
            for h in range(2):
                rows = slice(h * DH, h * DH + DH)
                sp.dma_start(vbd[rows, s, :, h * C:h * C + C], v_d[b, rows]).then_inc(kv_in[s], 16)

        sp.wait_ge(vbd_zero, 1)
        load_kv(0, 0)
        load_kv(1, 1)
        sp.dma_start(xres[:, 0], x_t[0]).then_inc(xres_in[0], 16)

        def step(i, u):
            n = i * BODY + u
            if u % TPB == 0 and valid(i, u, 2 * TPB):
                b = i * 2 + u // TPB
                sp.wait_ge(side_full, prep_job(i, u, "U3").count)
                load_kv(b + 2, u // TPB)
            if valid(i, u, 8):
                sp.wait_ge(xn_ready, n + 5)
                sp.dma_start(xin[:, u % 4], x_t[n + 8]).then_inc(xin_in[u % 4], 16)
            if valid(i, u, 1):
                if after_first(i, u):
                    unloaded(sp, side_job(i, u - 1, "O"))
                sp.dma_start(xres[:, (u + 1) % 2], x_t[n + 1]).then_inc(xres_in[(u + 1) % 2], 16)
            if valid(i, u, -2):
                unloaded(sp, side_job(i, u - 2, "O"))
                sp.dma_start(x1_d[n - 2], x1[:, u % 2]).then_inc(x1_stored[u % 2], 16)
                unloaded(sp, side_job(i, u - 1, "XT"))
                sp.dma_start(xn2T_d[n - 2], xn2T[:, u % 2]).then_inc(xn2T_stored[u % 2], 16)
            if u % TPB == 2 and valid(i, u, -3):
                b = i * 2 + (u - 6) // TPB
                sp.wait_ge(comb_ready, b + 1)
                s = (u - 6) // TPB % 2
                for t in range(TPB):
                    sp.dma_start(comb_d[b * TPB + t], comb[:, s, t]).then_inc(comb_stored[s], 16)

        turns(sp, BODY, TURNS, 3, step)
        for s in range(2):
            sp.wait_ge(x1_stored[s], 16 * TILES // 2)
            sp.wait_ge(xn2T_stored[s], 16 * TILES // 2)
            sp.wait_ge(comb_stored[s], 16 * TPB * B // 2)

    @block.tensor
    def _(pe):
        pe.wait_ge(wkv_in, 48)
        for j in range(4 * PAIRS):
            w, pair, half = (wk_s, wv_s)[j // (2 * PAIRS)], j // 2 % PAIRS, j % 2
            if j >= 4:
                pe.wait_ge(proj_read, j - 3)
            for k in range(KD):
                mm = pe.matmul(S[:, j // 2 % 2, j % 2 * N:j % 2 * N + N], w[:, k, pair * P:pair * P + P],
                               ctx_s[:, k, half * N:half * N + N], start=(k == 0), stop=(k == KD - 1))
            mm.then_inc(proj_full, 1)
        pe.wait_ge(proj_read, 4 * PAIRS)
        pe.wait_ge(consts_in, CONSTS)
        pe.wait_ge(consts_set, 1)

        def prepare(name, s, job, tiles, loads):
            j, o = int(name[1]), side[:, job.bank]
            bank_free(pe, job)
            if name[0] == "T":
                pe.wait_ge(xn_ready, tiles)
                for t in range(TPB):
                    mm = pe.transpose(o[:, t * P:t * P + P], xn[:, s, t, j * P:j * P + P], ident[:])
            elif name[0] == "G":
                k, h = j // 2, j % 2
                rows = slice(h * DH, h * DH + DH)
                pe.wait_ge(kv_in[s], loads)
                for pair in range(PAIRS):
                    mm = pe.matmul(o[:, pair * C:pair * C + C], wqT[rows, pair, k * P:k * P + P],
                                   keys[rows, s, pair, :], start=True, stop=True)
            else:
                pe.wait_ge(kv_in[s], loads)
                for q in range(2):
                    mm = pe.matmul(o[:, q * D:q * D + D], vbd[:, s, 2 * j + q, :], wo_s[:, 2 * j + q, :],
                                   start=True, stop=True)
            mm.then_inc(side_full, 1)


        def scores(u):
            s, t = u // TPB % 2, u % TPB
            for half in range(2):
                for k in range(KD):
                    mm = pe.matmul(S[:, u % 2, half * N:half * N + N], xnT[:, s, k, t * P:t * P + P],
                                   G[:, s, k, half * N:half * N + N], start=(k == 0), stop=(k == KD - 1))
            mm.then_inc(S_full, 1)

        for name in PREP_ORDER:
            prepare(name, 0, prep_job(0, 0, name), TPB, 48)
        unloaded(pe, prep_job(0, 0, "U2"))
        unloaded(pe, prep_job(0, 0, "U3"))
        scores(0)

        def step(i, u):
            n = i * BODY + u
            if valid(i, u, 1):
                if after_first(i, u):
                    pe.wait_ge(shifted, n)
                scores(u + 1)
            if prepares(i, u):
                q = u // TPB + 1
                for name in QUARTER[u % TPB]:
                    prepare(name, q % 2, side_job(i, u, name), i * BODY + (TPB * q + TPB), i * 48 + (48 * (q // 2) + 48))
            if valid(i, u, -2):
                job = side_job(i, u, "RT")
                bank_free(pe, job)
                unloaded(pe, side_job(i, u - 1, "XT"))
                for k in range(KD):
                    mm = pe.matmul(side[:, job.bank, 0:E], xn2T[:, u % 2, k, :], gate[:, k, :],
                                   start=(k == 0), stop=(k == KD - 1))
                mm.then_inc(side_full, 1)
            if valid(i, u, 0):
                pe.wait_ge(probs_ready, n + 1)
                if after_first(i, u):
                    pe.wait_ge(probsT_ready, n * 2)
                for pair in range(PAIRS):
                    mm = pe.transpose(PT[:, pair, :], probs[:, u % 2, pair * P:pair * P + P], ident[:])
                    if pair % 4 == 3:
                        mm.then_inc(PT_full, 1)
                job = side_job(i, u, "O")
                bank_free(pe, job)
                pe.wait_ge(probsT_ready, n * 2 + 2)
                for pair in range(PAIRS):
                    mm = pe.matmul(side[:, job.bank, 0:D], probsT[:, u % 2, pair, :], U[:, u // TPB % 2, pair, :],
                                   start=(pair == 0), stop=(pair == PAIRS - 1))
                mm.then_inc(side_full, 1)
            if valid(i, u, -1):
                job = side_job(i, u, "XT")
                bank_free(pe, job)
                pe.wait_ge(xn2_ready, n)
                for k in range(KD):
                    mm = pe.transpose(side[:, job.bank, k * P:k * P + P], xn2[:, (u - 1) % 2, k * P:k * P + P], ident[:])
                mm.then_inc(side_full, 1)

        turns(pe, BODY, TURNS, 3, step)

    @block.scalar
    def _(act):
        for j in range(4 * PAIRS):
            act.wait_ge(proj_full, j + 1)
            if j >= 4:
                act.wait_ge(kv_stored[j % 4], 16 * (j // 4))
            act.mul(kv_stage[:, j % 4], S[:, j // 2 % 2, j % 2 * N:j % 2 * N + N],
                    SCALE if j < 2 * PAIRS else 1.0).then_inc(proj_read, 1)

        def unload(name, s, job):
            j, o = int(name[1]), side[:, job.bank]
            act.wait_ge(side_full, job.count)
            if name[0] == "T":
                act.copy(xnT[:, s, j, :], o).then_inc(side_read[job.bank], 1)
            elif name[0] == "G":
                k, h = j // 2, j % 2
                act.copy(G[:, s, k].rearrange("p (r h c) -> p r h c", h=2, c=C)[:, :, h, :],
                         o.rearrange("p (r c) -> p r c", c=C)).then_inc(side_read[job.bank], 1)
            else:
                act.copy(U[:, s, 2 * j:2 * j + 2, :], o.rearrange("p (q d) -> p q d", q=2))\
                   .then_inc(side_read[job.bank], 1)

        def exponentials(u, tiles):
            act.wait_ge(shifted, tiles)
            act.activation(probs[:, u % 2], probs[:, u % 2], ACT.Exp).then_inc(exp_done, 1)

        for name in PREP_ORDER:
            unload(name, 0, prep_job(0, 0, name))
        exponentials(0, 1)

        def step(i, u):
            n = i * BODY + u
            if prepares(i, u):
                for name in QUARTER[u % TPB]:
                    unload(name, (u // TPB + 1) % 2, side_job(i, u, name))
            if valid(i, u, 0):
                for half in range(2):
                    act.wait_ge(PT_full, n * 2 + (half + 1))
                    pairs = slice(half * PAIRS // 2, (half + 1) * PAIRS // 2)
                    act.copy(probsT[:, u % 2, pairs], PT[:, pairs]).then_inc(probsT_ready, 1)
            if valid(i, u, 1):
                exponentials(u + 1, n + 2)
            if valid(i, u, -1):
                job = side_job(i, u, "XT")
                act.wait_ge(side_full, job.count)
                if valid(i, u, -3):
                    act.wait_ge(xn2T_stored[(u - 1) % 2], i * (8 * BODY) + 16 * ((u - 1) // 2))
                act.copy(xn2T[:, (u - 1) % 2], side[:, job.bank, 0:D].rearrange("p (k t) -> p k t", k=KD))\
                   .then_inc(side_read[job.bank], 1)

        turns(act, BODY, TURNS, 3, step)

    @block.gpsimd
    def _(pool):
        pool.memset(vbd[:], 0.0).then_inc(vbd_zero, 1)
        pool.memset(minus_half[:], -0.5)
        pool.memset(eps[:], EPS)
        pool.memset(base_e[:], BASE_E)
        pool.memset(ident[:], 0.0).then_inc(ident_zero, 1)
        pool.wait_ge(ident_zero, 1)
        pool.affine_select(out=ident[:], in_=ident[:], compare_op=ALU.not_equal, fill=1.0, base=0,
                           pattern=[[-1, P]], channel_multiplier=1).then_inc(consts_set, 1)

        def reciprocal_deviation(slot, norms, steps):
            pool.wait_ge(stats_ready, steps)
            pool.tensor_tensor(veps[:, slot, norms], mv[:, slot, norms, 1], eps[:, norms], ALU.add).then_inc(veps_ready, 1)
            pool.wait_ge(veps_ready, steps)
            pool.tensor_tensor(rstd[:, slot, norms], veps[:, slot, norms], minus_half[:, norms], ALU.pow)\
                .then_inc(rstd_ready, 1)

        def residual(u, loads):
            pool.wait_ge(xres_in[u % 2], loads)
            pool.tensor_tensor(xres[:, u % 2], xres[:, u % 2], bo_b[:], ALU.add).then_inc(residual_ready, 1)

        for m in range(8):
            reciprocal_deviation(m % 2, slice(1, 2), m + 1)
        pool.wait_ge(consts_in, CONSTS)
        residual(0, 16)

        def step(i, u):
            n = i * BODY + u
            norms = slice(0 if valid(i, u, -1) else 1, 2 if valid(i, u, 8) else 1)
            if norms.start < norms.stop:
                reciprocal_deviation(u % 2, norms, n + 9)
            if valid(i, u, 1):
                residual(u + 1, i * (8 * BODY) + 16 * ((u + 1) // 2 + 1))
            if valid(i, u, -2):
                unloaded(pool, side_job(i, u, "RT"))
                if u % TPB == 2 and valid(i, u, -2 - 2 * TPB):
                    pool.wait_ge(comb_ready, i * 2 + ((u - 2) // TPB - 1))
                pool.tensor_tensor(explog[:, (u - 2) // TPB % 2, (u - 2) % TPB], base_e[:], neglog[:, u % 2], ALU.pow)\
                    .then_inc(explog_ready, 1)

        turns(pool, BODY, TURNS, 3, step)

    @block.vector
    def _(dve):
        def wait_on_copy(sem, value, of):
            dve.wait_ge(sem, value)
            dve.tensor_copy(waited[:, 0:of.shape[1]], of)

        def first_stats(u, loads):
            dve.wait_ge(xin_in[u % 4], loads)
            return dve.bn_stats(bn[:, u % 2, 1], xin[:, u % 4])

        def normalise(to, of, slot, norm):
            return dve.tensor_scalar(to, of, mv[:, slot, norm, 0:1], rstd[:, slot, norm:norm + 1], ALU.subtract, ALU.mult)

        def shift(u, tiles):
            scores = S[:, u % 2].rearrange("p (h c) -> p h c", c=C)
            dve.wait_ge(S_full, tiles)
            dve.tensor_reduce(rowmax[:, u % 2], scores, AX.X, ALU.max).then_inc(max_ready, 1)
            dve.wait_ge(max_ready, tiles)
            dve.tensor_tensor(probs[:, u % 2].rearrange("p (h c) -> p h c", c=C), scores,
                              rowmax[:, u % 2].unsqueeze(2).to_broadcast([P, H, C]), ALU.subtract).then_inc(shifted, 1)

        def divide(u, tiles):
            p = probs[:, u % 2].rearrange("p (h c) -> p h c", c=C)
            dve.wait_ge(exp_done, tiles)
            dve.tensor_reduce(rowsum[:, u % 2], p, AX.X, ALU.add).then_inc(sum_ready, 1)
            dve.wait_ge(sum_ready, tiles)
            dve.reciprocal(rowinv[:, u % 2], rowsum[:, u % 2]).then_inc(inv_ready, 1)
            dve.wait_ge(inv_ready, tiles)
            dve.tensor_tensor(p, p, rowinv[:, u % 2].unsqueeze(2).to_broadcast([P, H, C]), ALU.mult)\
               .then_inc(probs_ready, 1)

        for m in range(8):
            first_stats(m, 16 * (m // 4 + 1)).then_inc(bn_done, 1)
            dve.wait_ge(bn_done, m + 1)
            dve.bn_aggr(mv[:, m % 2, 1], bn[:, m % 2, 1]).then_inc(stats_ready, 1)
            dve.wait_ge(rstd_ready, m + 1)
            normalise(xn[:, m // TPB, m % TPB], xin[:, m % 4], m % 2, 1).then_inc(xn_ready, 1)
        dve.wait_ge(consts_in, CONSTS)
        shift(0, 1)
        divide(0, 1)

        def route(s, b, have_before):
            dve.wait_ge(explog_ready, b * TPB + TPB)
            dve.tensor_scalar(denom[:], explog[:, s], 1.0, None, ALU.add).then_inc(scored, 1)
            dve.wait_ge(scored, b * 2 + 1)
            dve.reciprocal(score[:], denom[:]).then_inc(scored, 1)
            dve.wait_ge(scored, b * 2 + 2)
            dve.tensor_tensor(biased[:], score[:], gb_b[:], ALU.add).then_inc(biased_ready, 1)
            wait_on_copy(biased_ready, b + 1, biased[:, 0:1, 0:1])
            for t in range(TPB):
                top = dve.max(top8[:, t], biased[:, t])
            top.then_inc(top_ready, 1)
            dve.wait_ge(top_ready, b * 2 + 1)
            dve.memset(top8[:, :, TOPK:8], NEVER).then_inc(top_ready, 1)
            wait_on_copy(top_ready, b * 2 + 2, top8[:, 0:1, 0:1])
            for t in range(TPB):
                top = dve.match_replace(rest[:, t], top8[:, t], biased[:, t], -NEVER)
            top.then_inc(picked_ready, 1)
            dve.wait_ge(picked_ready, b * 2 + 1)
            dve.tensor_tensor(picked[:], rest[:], biased[:], ALU.not_equal).then_inc(picked_ready, 1)
            dve.wait_ge(picked_ready, b * 2 + 2)
            dve.tensor_tensor(weight[:], picked[:], score[:], ALU.mult).then_inc(weight_ready, 1)
            dve.wait_ge(weight_ready, b + 1)
            dve.tensor_reduce(wsum[:], weight[:], AX.X, ALU.add).then_inc(wsum_ready, 1)
            dve.wait_ge(wsum_ready, b * 2 + 1)
            dve.reciprocal(winv[:], wsum[:]).then_inc(wsum_ready, 1)
            dve.wait_ge(wsum_ready, b * 2 + 2)
            if have_before:
                dve.wait_ge(comb_stored[s], (b - s) * (8 * TPB))
            dve.scalar_tensor_tensor(out=comb[:, s], in0=weight[:], scalar=ROUTE_SCALE,
                                     in1=winv[:].unsqueeze(2).to_broadcast([P, TPB, E]), op0=ALU.mult, op1=ALU.mult)\
               .then_inc(comb_ready, 1)

        def step(i, u):
            n = i * BODY + u
            second, first = valid(i, u, -1), valid(i, u, 8)
            norms = slice(0 if second else 1, 2 if first else 1)
            if second:
                job = side_job(i, u - 1, "O")
                s = (u - 1) % 2
                dve.wait_ge(side_full, job.count)
                dve.wait_ge(residual_ready, n)
                if valid(i, u, -3):
                    dve.wait_ge(x1_stored[s], i * (8 * BODY) + 16 * ((u - 1) // 2))
                dve.tensor_tensor(x1[:, s], side[:, job.bank, 0:D], xres[:, s], ALU.add).then_inc(side_read[job.bank], 1)
                unloaded(dve, job)
                last = dve.bn_stats(bn[:, u % 2, 0], x1[:, s])
            if first:
                last = first_stats(u, i * 32 + 16 * (u // 4 + 3))
            if second or first:
                last.then_inc(bn_done, 1)
                wait_on_copy(bn_done, n + 9, bn[:, u % 2, norms, 0:1])
                if second:
                    last = dve.bn_aggr(mv[:, u % 2, 0], bn[:, u % 2, 0])
                if first:
                    last = dve.bn_aggr(mv[:, u % 2, 1], bn[:, u % 2, 1])
                last.then_inc(stats_ready, 1)
            if valid(i, u, 1):
                shift(u + 1, n + 2)
            if second or first:
                dve.wait_ge(rstd_ready, n + 9)
            if second:
                normalise(xn2[:, (u - 1) % 2], x1[:, (u - 1) % 2], u % 2, 0).then_inc(xn2_ready, 1)
            if first:
                normalise(xn[:, u // TPB % 2, u % TPB], xin[:, u % 4], u % 2, 1).then_inc(xn_ready, 1)
            if valid(i, u, 1):
                divide(u + 1, n + 2)
            if valid(i, u, -2):
                job = side_job(i, u, "RT")
                dve.wait_ge(side_full, job.count)
                if valid(i, u, -4):
                    dve.wait_ge(explog_ready, n - 3)
                dve.tensor_scalar(neglog[:, u % 2], side[:, job.bank, 0:E], -1.0, None, ALU.mult)\
                   .then_inc(side_read[job.bank], 1)
            if u % TPB == 2 and valid(i, u, -3):
                route((u - 3) // TPB % 2, i * 2 + (u - 3) // TPB, valid(i, u, -3 - 2 * TPB))

        turns(dve, BODY, TURNS, 3, step)


JOBS = (EA + 1) // 2
B_BODY = 2 * JOBS
B_TURNS = TILES // 2


def phase_b(nc, ctx, w13, w2, w13_s, w2_s, ident, scratch, out_t):
    x1_d, xn2T_d, comb_d = (scratch[k] for k in ("x1", "xn2T", "comb"))

    def sb(name, shape, dt=F32):
        return ctx.enter_context(nc.sbuf_tensor(name, shape, dt))

    def sem(name):
        return ctx.enter_context(nc.semaphore(name))

    w13_hl = sb("w13_hl", [P, KD, 2, EA * 2 * I], F32R)
    w2_hl = sb("w2_hl", [P, EA, 2, D], F32R)
    stage = sb("stage", [P, 2, 3, D])
    xT = sb("xT", [P, 2, KD, P])
    xT_hl = sb("xT_hl", [P, 2, 2, KD, P], F32R)
    x1 = sb("x1_b", [P, 2, D])
    cw = sb("cw", [P, 2, E])
    gated = sb("gated", [P, 2, 2, I])
    hid = sb("hid", [P, 2, 2, I])
    hidT_hl = sb("hidT_hl", [P, 2, 2, 2 * P], F32R)
    part = sb("part", [P, D])
    y = sb("y", [P, 2, D])
    UP = ctx.enter_context(nc.psum_tensor("UP", [P, 3, 4 * I], F32))
    HT = ctx.enter_context(nc.psum_tensor("HT", [P, 3, 4 * P], F32))
    Y = ctx.enter_context(nc.psum_tensor("Y", [P, 2, 2 * D], F32))

    stage_in = [sem("stage_in0"), sem("stage_in1")]
    w_high = sem("w_high")
    w_low = sem("w_low")
    xT_in = [sem("xT_in0"), sem("xT_in1")]
    rest_in = [sem("rest_in0"), sem("rest_in1")]
    x_high = sem("x_high")
    x_low = sem("x_low")
    up_full = sem("up_full")
    gated_ready = sem("gated_ready")
    hid_ready = sem("hid_ready")
    ht_full = sem("ht_full")
    ht_high = sem("ht_high")
    ht_low = sem("ht_low")
    y_full = sem("y_full")
    part_ready = sem("part_ready")
    y_ready = sem("y_ready")
    y_stored = [sem("y_stored0"), sem("y_stored1")]
    block = ctx.enter_context(nc.Block())

    def ok(i, v, d):
        return 0 <= i * B_BODY + v + d < TILES * JOBS if isinstance(i, int) else True

    def tile_ok(i, u, d):
        return 0 <= i * 2 + u + d < TILES if isinstance(i, int) else True

    def some(value):
        return not isinstance(value, int) or value > 0

    @block.sync
    def _(sp):
        for e in range(EA):
            s = e % 2
            if e >= 2:
                sp.wait_ge(w_low, 2 * e - 2)
            a, b = (w13[:, e], w2[:, e]) if e < E else (w13_s, w2_s)
            sp.dma_start(stage[:, s, 0:KD], a.rearrange("(k p) n -> p k n", p=P)).then_inc(stage_in[s], 16)
            sp.dma_start(stage[:, s, KD], b).then_inc(stage_in[s], 16)

        def load_xT(u, n):
            sp.dma_start(xT[:, u % 2], xn2T_d[n]).then_inc(xT_in[u % 2], 16)

        def load_rest(u, n):
            sp.dma_start(x1[:, u % 2], x1_d[n]).then_inc(rest_in[u % 2], 16)
            sp.dma_start(cw[:, u % 2], comb_d[n]).then_inc(rest_in[u % 2], 16)

        load_xT(0, 0)
        load_xT(1, 1)
        load_rest(0, 0)

        def step(i, u):
            n = i * 2 + u
            if tile_ok(i, u, -1):
                sp.wait_ge(y_ready, n)
                sp.dma_start(out_t[n - 1], y[:, (u - 1) % 2]).then_inc(y_stored[(u - 1) % 2], 16)
            if tile_ok(i, u, 1):
                load_rest(u + 1, n + 1)
            if tile_ok(i, u, 2):
                sp.wait_ge(x_low, n + 1)
                load_xT(u, n + 2)

        turns(sp, 2, B_TURNS, 1, step)
        for s in range(2):
            sp.wait_ge(y_stored[s], 16 * TILES // 2)

    @block.tensor
    def _(pe):
        pe.wait_ge(w_high, 2 * EA)
        pe.wait_ge(w_low, 2 * EA)

        def step(i, v):
            g = i * B_BODY + v
            if ok(i, v, 0):
                n, j, s = i * 2 + v // JOBS, v % JOBS, v // JOBS % 2
                if j == 0:
                    pe.wait_ge(x_low, n + 1)
                if some(g - 2):
                    pe.wait_ge(hid_ready, g - 2)
                cols = slice(2 * j * 2 * I, min(2 * j + 2, EA) * 2 * I)
                width = cols.stop - cols.start
                passes = [(xh, wh, k) for xh, wh in ((0, 0), (0, 1), (1, 0)) for k in range(KD)]
                for xh, wh, k in passes:
                    mm = pe.matmul(UP[:, v % 3, 0:width], xT_hl[:, s, xh, k], w13_hl[:, k, wh, cols],
                                   start=((xh, wh, k) == passes[0]), stop=((xh, wh, k) == passes[-1]))
                mm.then_inc(up_full, 1)
            if ok(i, v, -1):
                if some(g - 3):
                    pe.wait_ge(ht_low, g - 3)
                pe.wait_ge(hid_ready, g)
                for q in range(1 if (v - 1) % JOBS == JOBS - 1 else 2):
                    mm = pe.transpose(HT[:, (v - 1) % 3, q * P:q * P + P], hid[:, (v - 1) % 2, q], ident[:])
                mm.then_inc(ht_full, 1)
            if ok(i, v, -2):
                n, j, s = i * 2 + (v - 2) // JOBS, (v - 2) % JOBS, (v - 2) // JOBS % 2
                if j == 0 and tile_ok(i, (v - 2) // JOBS, -2):
                    pe.wait_ge(y_ready, n - 1)
                pe.wait_ge(ht_low, g - 1)
                for q in range(1 if j == JOBS - 1 else 2):
                    e, last = 2 * j + q, j == JOBS - 1
                    pe.matmul(Y[:, s], hidT_hl[:, v % 2, 0, q * P:q * P + P], w2_hl[:, e].rearrange("p a d -> p (a d)"),
                              start=(e == 0), stop=last)
                    mm = pe.matmul(Y[:, s, 0:D], hidT_hl[:, v % 2, 1, q * P:q * P + P], w2_hl[:, e, 0],
                                   start=False, stop=last, skip_group_check=True)
                if j == JOBS - 1:
                    mm.then_inc(y_full, 1)

        turns(pe, B_BODY, B_TURNS, 3, step)

    @block.scalar
    def _(act):
        for e in range(EA):
            s = e % 2
            act.wait_ge(stage_in[s], 32 * (e // 2 + 1))
            act.copy(w13_hl[:, :, 0, e * 2 * I:(e + 1) * 2 * I], stage[:, s, 0:KD]).then_inc(w_high, 1)
            act.copy(w2_hl[:, e, 0], stage[:, s, KD]).then_inc(w_high, 1)

        def split(u, tiles, loads):
            act.wait_ge(xT_in[u % 2], loads)
            act.copy(xT_hl[:, u % 2, 0], xT[:, u % 2]).then_inc(x_high, 1)

        split(0, 1, 16)

        def step(i, v):
            g = i * B_BODY + v
            if ok(i, v, 0):
                j = v % JOBS
                width = 1 if j == JOBS - 1 else 2
                act.wait_ge(up_full, g + 1)
                if some(g - 1):
                    act.wait_ge(hid_ready, g - 1)
                up = UP[:, v % 3].rearrange("p (q s i) -> p q s i", q=2, s=2)
                act.activation(gated[:, v % 2, 0:width], up[:, 0:width, 0], ACT.Silu).then_inc(gated_ready, 1)
                if j == 4 and tile_ok(i, v // JOBS, 1):
                    u = v // JOBS + 1
                    split(u, 0, i * 16 + 16 * (u // 2 + 1))
            if ok(i, v, -1):
                width = 1 if (v - 1) % JOBS == JOBS - 1 else 2
                act.wait_ge(ht_full, g)
                act.copy(hidT_hl[:, (v - 1) % 2, 0, 0:width * P], HT[:, (v - 1) % 3, 0:width * P]).then_inc(ht_high, 1)

        turns(act, B_BODY, B_TURNS, 3, step)

    @block.vector
    def _(dve):
        for e in range(EA):
            s = e % 2
            dve.wait_ge(w_high, 2 * e + 2)
            high = w13_hl[:, :, 0, e * 2 * I:(e + 1) * 2 * I]
            dve.tensor_tensor(w13_hl[:, :, 1, e * 2 * I:(e + 1) * 2 * I], stage[:, s, 0:KD], high.bitcast(F32), ALU.subtract)\
               .then_inc(w_low, 1)
            dve.tensor_tensor(w2_hl[:, e, 1], stage[:, s, KD], w2_hl[:, e, 0].bitcast(F32), ALU.subtract).then_inc(w_low, 1)

        def split(u, tiles):
            dve.wait_ge(x_high, tiles)
            dve.tensor_tensor(xT_hl[:, u % 2, 1], xT[:, u % 2], xT_hl[:, u % 2, 0].bitcast(F32), ALU.subtract).then_inc(x_low, 1)

        split(0, 1)

        def step(i, v):
            g = i * B_BODY + v
            if ok(i, v, 0):
                j, u = v % JOBS, v // JOBS
                if j == 0:
                    dve.wait_ge(rest_in[u % 2], i * 32 + 32)
                dve.wait_ge(gated_ready, g + 1)
                if some(g - 1):
                    dve.wait_ge(ht_full, g - 1)
                up = UP[:, v % 3].rearrange("p (q s i) -> p q s i", q=2, s=2)
                if j == JOBS - 1:
                    last = dve.tensor_tensor(hid[:, v % 2, 0], up[:, 0, 1], gated[:, v % 2, 0], ALU.mult)
                else:
                    for q in range(2):
                        e = 2 * j + q
                        last = dve.scalar_tensor_tensor(out=hid[:, v % 2, q], in0=up[:, q, 1], scalar=cw[:, u % 2, e:e + 1],
                                                        in1=gated[:, v % 2, q], op0=ALU.mult, op1=ALU.mult)
                last.then_inc(hid_ready, 1)
                if j == 4 and tile_ok(i, u, 1):
                    split(u + 1, i * 2 + (u + 2))
            if ok(i, v, -1):
                width = 1 if (v - 1) % JOBS == JOBS - 1 else 2
                dve.wait_ge(ht_high, g)
                dve.tensor_tensor(hidT_hl[:, (v - 1) % 2, 1, 0:width * P], HT[:, (v - 1) % 3, 0:width * P],
                                  hidT_hl[:, (v - 1) % 2, 0, 0:width * P].bitcast(F32), ALU.subtract).then_inc(ht_low, 1)
            if v % JOBS == 2 and tile_ok(i, v // JOBS, -1):
                u = v // JOBS - 1
                n = i * 2 + u
                dve.wait_ge(y_full, n + 1)
                dve.tensor_tensor(part[:], Y[:, u % 2, 0:D], x1[:, u % 2], ALU.add).then_inc(part_ready, 1)
                dve.wait_ge(part_ready, n + 1)
                if tile_ok(i, u, -2):
                    dve.wait_ge(y_stored[u % 2], i * 16 + 16 * (u // 2))
                dve.tensor_tensor(y[:, u % 2], Y[:, u % 2, D:2 * D], part[:], ALU.add).then_inc(y_ready, 1)

        turns(dve, B_BODY, B_TURNS, 3, step)


def kernel(**inputs):
    import numpy as np
    import concourse.bacc as bacc
    from concourse.bass_utils import run_bass_kernel_spmd

    a = {k: np.asarray(v) for k, v in inputs.items()}
    arrays = {
        "x": a["x"],
        "ctxT": a["ctx_1024"].reshape(B * C, D).T,
        "wq": a["L0_xattn_Wq"].T,
        "wk": a["L0_xattn_Wk"],
        "wv": a["L0_xattn_Wv"],
        "wo": a["L0_xattn_Wo"],
        "bo": a["L0_xattn_bo"],
        "gateT": a["L0_ffn_gate_w"].T,
        "gate_b": a["L0_ffn_gate_b"],
        "w13": a["L0_ffn_w13"].transpose(2, 0, 1),
        "w2": a["L0_ffn_w2"].transpose(2, 0, 1),
        "w13_s": a["L0_ffn_w13_s"].T,
        "w2_s": a["L0_ffn_w2_s"].T,
    }
    nc = bacc.Bacc("TRN2", target_bir_lowering=False, num_devices=1)
    feeds, args = {}, {}
    for name, value in arrays.items():
        value = np.ascontiguousarray(value)
        feeds[f"in_{name}"] = value
        args[name] = nc.dram_tensor(f"in_{name}", value.shape, mybir.dt.from_np(value.dtype), kind="ExternalInput").ap()
    args["out"] = nc.dram_tensor("out_y", (B, N, D), F32, kind="ExternalOutput").ap()
    build(nc, **args)
    r = run_bass_kernel_spmd(nc, [feeds], core_ids=[0])
    return r.results[0]["out_y"]
```

```python
from contextlib import ExitStack

import concourse.bass as bass
from concourse import mybir

F32 = mybir.dt.float32
F32R = mybir.dt.float32r
I32 = mybir.dt.int32
U32 = mybir.dt.uint32
ALU = mybir.AluOpType
ACT = mybir.ActivationFunctionType
AX = mybir.AxisListType

P = 128
B, N, D = 16, 512, 256
H, DH = 16, 64
C = 64
KD = D // P
PAIRS = H // 2
HC = H * C
TILES = B * N // P
TPB = N // P
E, I, TOPK = 16, 128, 4
EA = E + 1
SCALE = DH ** -0.5
ROUTE_SCALE = 2.5
TOK = B * N
STEP = 2 * P
ROOM = TOK + STEP
ROW = D + 1 + EA
ID, CW = D, D + 1
E_BODY = 8
STEPS = (TOK * TOPK + E * (STEP - 1)) // STEP + TOK // STEP
STEPS += -STEPS % E_BODY
SUMS = TOK + STEP
EPS = 1e-5
BODY = 2 * TPB
DRAIN = 6
TURNS = TILES // BODY
NEVER = 3.0e38


def build(nc, x, ctxT, wq, wk, wv, wo, bo, gateT, gate_b, w13, w2, w13_s, w2_s, sums):
    x_t = x.rearrange("b (t p) d -> (b t) p d", p=P)
    scratch = {
        "k": nc.dram_tensor("keys_scratch", [B, P, PAIRS, C], F32).ap(),
        "v": nc.dram_tensor("values_scratch", [B, P, PAIRS, C], F32).ap(),
        "queue": nc.dram_tensor("queue_scratch", [EA * ROOM + STEP, ROW], F32).ap(),
        "table": nc.dram_tensor("table_scratch", [3, 2 * P], I32).ap(),
        "ends": nc.dram_tensor("ends_scratch", [EA, 1], I32).ap(),
    }
    with ExitStack() as outer:
        ident = outer.enter_context(nc.sbuf_tensor("ident", [P, P], F32))
        ones = outer.enter_context(nc.sbuf_tensor("ones", [P, P], F32))
        counts = outer.enter_context(nc.sbuf_tensor("counts", [P, EA], F32))
        with ExitStack() as ctx:
            phase_a(nc, ctx, x_t, ctxT, wq, wk, wv, wo, bo, gateT, gate_b, ident, ones, counts, scratch, sums)
        with ExitStack() as ctx:
            phase_t(nc, ctx, ident, ones, counts, scratch)
        with ExitStack() as ctx:
            phase_e(nc, ctx, w13, w2, w13_s, w2_s, ident, scratch, sums)


def turns(eng, body, count, drain, step):
    for u in range(body):
        step(0, u)
    with eng.Fori(1, count - 1) as i:
        for u in range(body):
            step(i, u)
    for u in range(body):
        step(count - 1, u)
    for u in range(drain):
        step(count, u)


QUARTER = [["T0", "T1", "G0"], ["G1", "G2", "G3"], ["U0", "U1"], ["U2", "U3"]]
PREP_ORDER = ["T0", "T1", "G0", "G1", "G2", "G3", "U0", "U1", "U2", "U3"]
OWN = [("RT", 2), ("O", 0), ("XT", 1)]


def side_jobs(m):
    prep = QUARTER[m % TPB] if m + TPB - m % TPB < TILES else []
    own = [name for name, lag in OWN if 0 <= m - lag < TILES]
    return (["PL"] if m % 2 == 0 and 0 <= m - 6 < TILES else []) + list(prep) + own


def jobs_before(m):
    return len(PREP_ORDER) + sum(len(side_jobs(w)) for w in range(m))


TOK_PER_TURN = BODY * P
PER_TURN = jobs_before(3 * BODY) - jobs_before(2 * BODY)


class Job:

    def __init__(self, turn, at):
        self.count, self.before, self.bank = turn * PER_TURN + (at + 1), turn * (PER_TURN // 2) + at // 2, at % 2
        self.first = isinstance(turn, int) and turn == 0 and at < 2


def side_job(i, u, name):
    if isinstance(i, int):
        m = i * BODY + u
        return Job(0, jobs_before(m) + side_jobs(m).index(name))
    m = 2 * BODY + u
    return Job(i, jobs_before(m) + side_jobs(m).index(name) - 2 * PER_TURN)


def prep_job(i, u, name):
    if isinstance(i, int) and i * BODY + u < TPB:
        return Job(0, PREP_ORDER.index(name))
    quarter = [name in q for q in QUARTER].index(True)
    return side_job(i, u // TPB * TPB - TPB + quarter, name)


def valid(i, u, d):
    return 0 <= i * BODY + u + d < TILES if isinstance(i, int) else True


def prepares(i, u):
    return not isinstance(i, int) or i * BODY + u + TPB - u % TPB < TILES


def after_first(i, u):
    return not isinstance(i, int) or i * BODY + u >= 1


def phase_a(nc, ctx, x_t, ctxT, wq, wk, wv, wo, bo, gateT, gate_b, ident, ones, counts, scratch, sums):
    k_d, v_d, queue_d = (scratch[k] for k in ("k", "v", "queue"))
    x1_d = sums[0:TOK].rearrange("(n p) d -> n p d", p=P)
    shared_d = queue_d[E * ROOM:E * ROOM + TOK].rearrange("(n p) d -> n p d", p=P)

    def sb(name, shape, dt=F32):
        return ctx.enter_context(nc.sbuf_tensor(name, shape, dt))

    def sem(name):
        return ctx.enter_context(nc.semaphore(name))

    bo_b = sb("bo_b", [P, D])
    gb_b = sb("gb_b", [P, 2, E])
    gate = sb("gate", [P, KD, E])
    minus_half = sb("minus_half", [P, 2])
    eps = sb("eps", [P, 2])
    waited_pool = sb("waited_pool", [P, 1])
    waited = sb("waited", [P, 2, 1])
    wqT = sb("wqT", [P, PAIRS, D])
    wo_s = sb("wo_s", [P, PAIRS, D])
    wk_s = sb("wk_s", [P, KD, H * DH])
    wv_s = sb("wv_s", [P, KD, H * DH])
    ctx_s = sb("ctx_s", [P, KD, B * C])
    kv_stage = sb("kv_stage", [P, 4, N])
    xin = sb("xin", [P, 4, D])
    xres = sb("xres", [P, 2, D])
    xn = sb("xn", [P, 2, TPB, D])
    xnT = sb("xnT", [P, 2, KD, N])
    kbd = sb("kbd", [P, 2, PAIRS, P])
    vbd = sb("vbd", [P, 2, PAIRS, P])
    G = sb("G", [P, 2, KD, HC])
    U = sb("U", [P, 2, PAIRS, D])
    probs = sb("probs", [P, 2, HC])
    probsT = sb("probsT", [P, 2, PAIRS, P])
    x1 = sb("x1", [P, 2, D])
    rows = sb("rows", [P, BODY, ROW])
    zeros = sb("zeros", [P, STEP // P, D])
    xn2T = sb("xn2T", [P, 2, KD, P])
    rowmax = sb("rowmax", [P, 2, H])
    rowsum = sb("rowsum", [P, 2, H])
    rowinv = sb("rowinv", [P, 2, H])
    bn = sb("bn", [P, 2, 2, 6])
    mv = sb("mv", [P, 2, 2, 2])
    veps = sb("veps", [P, 2, 2])
    rstd = sb("rstd", [P, 2, 2])
    explog = sb("explog", [P, 2, 2, E])
    denom = sb("denom", [P, 2, E])
    score = sb("score", [P, 2, E])
    biased = sb("biased", [P, 2, E])
    top8 = sb("top8", [P, 2, 8])
    rest = sb("rest", [P, 2, E])
    picked = sb("picked", [P, 2, 2, E])
    before = sb("before", [P, 2, 2, E])
    weight = sb("weight", [P, 2, E])
    wsum = sb("wsum", [P, 2])
    winv = sb("winv", [P, 2])
    earlier = sb("earlier", [P, P])
    first_row_i = sb("first_row_i", [P, 2, E], I32)
    turn_i = sb("turn_i", [P, 1], I32)
    first_row = sb("first_row", [P, 2, E])
    place = sb("place", [P, 2, E])
    placed = sb("placed", [P, 2, E])
    place8 = sb("place8", [P, 2, 8])
    slots = sb("slots", [P, 2, 2, TOPK], U32)

    S = ctx.enter_context(nc.psum_tensor("S", [P, 2, HC], F32))
    PT = ctx.enter_context(nc.psum_tensor("PT", [P, PAIRS, P], F32))
    side = ctx.enter_context(nc.psum_tensor("side", [P, 2, N], F32))

    consts_in = sem("consts_in")
    wkv_in = sem("wkv_in")
    proj_full = sem("proj_full")
    proj_read = sem("proj_read")
    kv_stored = [sem(f"kv_stored{i}") for i in range(4)]
    xin_in = [sem(f"xin_in{i}") for i in range(4)]
    xres_in = [sem(f"xres_in{i}") for i in range(2)]
    kv_in = [sem(f"kv_in{i}") for i in range(2)]
    x1_stored = [sem(f"x1_stored{i}") for i in range(2)]
    queued = [sem(f"queued{i}") for i in range(BODY)]
    shared_queued = [sem(f"shared_queued{i}") for i in range(BODY)]
    zeros_set = sem("zeros_set")
    iota_set = sem("iota_set")
    tail_zeroed = sem("tail_zeroed")
    before_step = sem("before_step")
    place_step = sem("place_step")
    slots_ready = sem("slots_ready")
    counted = sem("counted")
    numbered = sem("numbered")
    ident_zero = sem("ident_zero")
    bd_zero = sem("bd_zero")
    consts_set = sem("consts_set")
    bn_done = sem("bn_done")
    stats_ready = sem("stats_ready")
    veps_ready = sem("veps_ready")
    rstd_ready = sem("rstd_ready")
    xn_ready = sem("xn_ready")
    xn2_ready = sem("xn2_ready")
    S_full = sem("S_full")
    max_ready = sem("max_ready")
    shifted = sem("shifted")
    exp_done = sem("exp_done")
    sum_ready = sem("sum_ready")
    inv_ready = sem("inv_ready")
    probs_ready = sem("probs_ready")
    residual_ready = sem("residual_ready")
    scored = sem("scored")
    biased_ready = sem("biased_ready")
    top_ready = sem("top_ready")
    picked_ready = sem("picked_ready")
    weight_ready = sem("weight_ready")
    wsum_ready = sem("wsum_ready")
    PT_full = sem("PT_full")
    probsT_ready = sem("probsT_ready")
    side_full = sem("side_full")
    side_read = [sem("side_read0"), sem("side_read1")]
    routed = sem("routed")
    CONSTS = 16 * (4 + 2)

    block = ctx.enter_context(nc.Block())

    def unloaded(eng, job):
        eng.wait_ge(side_read[job.bank], job.before + 1)

    def bank_free(eng, job):
        if not job.first:
            eng.wait_ge(side_read[job.bank], job.before)

    @block.sync
    def _(sp):
        for to, of in (wk_s, wk), (wv_s, wv):
            sp.dma_start(to[:], of.rearrange("(k p) n -> p k n", p=P)).then_inc(wkv_in, 16)
        sp.dma_start(ctx_s[:], ctxT.rearrange("(k p) n -> p k n", p=P)).then_inc(wkv_in, 16)
        for m in range(4):
            sp.dma_start(xin[:, m], x_t[m]).then_inc(xin_in[m], 16)
        sp.dma_start(wqT[:], wq.rearrange("(h p) n -> p h n", p=P)).then_inc(consts_in, 16)
        sp.dma_start(wo_s[:], wo.rearrange("(h p) n -> p h n", p=P)).then_inc(consts_in, 16)
        sp.dma_start(gate[:], gateT.rearrange("(k p) n -> p k n", p=P)).then_inc(consts_in, 16)
        sp.dma_start(bo_b[:], bo.rearrange("(a d) -> a d", a=1).to_broadcast([P, D])).then_inc(consts_in, 16)
        for t in range(2):
            sp.dma_start(gb_b[:, t], gate_b.rearrange("(a d) -> a d", a=1).to_broadcast([P, E])).then_inc(consts_in, 16)
        for m in range(4, 8):
            sp.wait_ge(xn_ready, m - 3)
            sp.dma_start(xin[:, m % 4], x_t[m]).then_inc(xin_in[m % 4], 16)
        for j in range(4 * PAIRS):
            to, pair, half = (k_d, v_d)[j // (2 * PAIRS)], j // 2 % PAIRS, j % 2
            sp.wait_ge(proj_read, j + 1)
            sp.dma_start(to[half * 8:half * 8 + 8, :, pair, :].rearrange("b p c -> p b c"),
                         kv_stage[:, j % 4].rearrange("p (b c) -> p b c", c=C)).then_inc(kv_stored[j % 4], 16)
        for s in range(4):
            sp.wait_ge(kv_stored[s], 16 * PAIRS)

        def load_kv(b, s):
            for h in range(2):
                rows = slice(h * DH, h * DH + DH)
                sp.dma_start(kbd[rows, s, :, h * C:h * C + C], k_d[b, rows]).then_inc(kv_in[s], 16)
                sp.dma_start(vbd[rows, s, :, h * C:h * C + C], v_d[b, rows]).then_inc(kv_in[s], 16)

        sp.wait_ge(bd_zero, 1)
        load_kv(0, 0)
        load_kv(1, 1)
        sp.dma_start(xres[:, 0], x_t[0]).then_inc(xres_in[0], 16)

        def step(i, u):
            n = i * BODY + u
            if u % TPB == 0 and valid(i, u, 2 * TPB):
                b = i * 2 + u // TPB
                sp.wait_ge(side_full, prep_job(i, u, "U3").count)
                load_kv(b + 2, u // TPB)
            if valid(i, u, 8):
                sp.wait_ge(xn_ready, n + 5)
                sp.dma_start(xin[:, u % 4], x_t[n + 8]).then_inc(xin_in[u % 4], 16)
            if valid(i, u, 1):
                if after_first(i, u):
                    unloaded(sp, side_job(i, u - 1, "O"))
                sp.dma_start(xres[:, (u + 1) % 2], x_t[n + 1]).then_inc(xres_in[(u + 1) % 2], 16)
            if valid(i, u, -2):
                unloaded(sp, side_job(i, u - 2, "O"))
                sp.dma_start(x1_d[n - 2], x1[:, u % 2]).then_inc(x1_stored[u % 2], 16)
            if valid(i, u, -7):
                m = (u - 7) % BODY
                sp.wait_ge(numbered, i * BODY + (u - 6))
                sp.dma_start(shared_d[n - 7], rows[:, m]).then_inc(shared_queued[m], 16)

        sp.wait_ge(zeros_set, 1)
        sp.dma_start(sums[TOK:SUMS].rearrange("(t p) d -> p t d", p=P), zeros[:]).then_inc(tail_zeroed, 16)
        turns(sp, BODY, TURNS, DRAIN + 1, step)
        for s in range(2):
            sp.wait_ge(x1_stored[s], 16 * TILES // 2)
        sp.wait_ge(tail_zeroed, 16)
        for m in range(BODY):
            sp.wait_ge(shared_queued[m], 16 * TURNS)

    @block.tensor
    def _(pe):
        pe.wait_ge(wkv_in, 48)
        for j in range(4 * PAIRS):
            w, pair, half = (wk_s, wv_s)[j // (2 * PAIRS)], j // 2 % PAIRS, j % 2
            if j >= 4:
                pe.wait_ge(proj_read, j - 3)
            for k in range(KD):
                mm = pe.matmul(S[:, j // 2 % 2, j % 2 * N:j % 2 * N + N], w[:, k, pair * P:pair * P + P],
                               ctx_s[:, k, half * N:half * N + N], start=(k == 0), stop=(k == KD - 1))
            mm.then_inc(proj_full, 1)
        pe.wait_ge(proj_read, 4 * PAIRS)
        pe.wait_ge(consts_in, CONSTS)
        pe.wait_ge(consts_set, 1)

        def prepare(name, s, job, tiles, loads):
            j, o = int(name[1]), side[:, job.bank]
            bank_free(pe, job)
            if name[0] == "T":
                pe.wait_ge(xn_ready, tiles)
                for t in range(TPB):
                    mm = pe.transpose(o[:, t * P:t * P + P], xn[:, s, t, j * P:j * P + P], ident[:])
            elif name[0] == "G":
                k, half = j // 2, j % 2
                pe.wait_ge(kv_in[s], loads)
                for q in range(PAIRS // 2):
                    pair = half * (PAIRS // 2) + q
                    mm = pe.matmul(o[:, q * P:q * P + P], wqT[:, pair, k * P:k * P + P], kbd[:, s, pair, :],
                                   start=True, stop=True)
            else:
                pe.wait_ge(kv_in[s], loads)
                for q in range(2):
                    mm = pe.matmul(o[:, q * D:q * D + D], vbd[:, s, 2 * j + q, :], wo_s[:, 2 * j + q, :],
                                   start=True, stop=True)
            mm.then_inc(side_full, 1)


        def scores(u):
            s, t = u // TPB % 2, u % TPB
            for half in range(2):
                for k in range(KD):
                    mm = pe.matmul(S[:, u % 2, half * N:half * N + N], xnT[:, s, k, t * P:t * P + P],
                                   G[:, s, k, half * N:half * N + N], start=(k == 0), stop=(k == KD - 1))
            mm.then_inc(S_full, 1)

        for name in PREP_ORDER:
            prepare(name, 0, prep_job(0, 0, name), TPB, 64)
        unloaded(pe, prep_job(0, 0, "U2"))
        unloaded(pe, prep_job(0, 0, "U3"))
        scores(0)
        scores(1)

        def step(i, u):
            n = i * BODY + u
            if valid(i, u, 0):
                pe.wait_ge(probs_ready, n + 1)
                if after_first(i, u):
                    pe.wait_ge(probsT_ready, n * 2)
                for pair in range(PAIRS):
                    mm = pe.transpose(PT[:, pair, :], probs[:, u % 2, pair * P:pair * P + P], ident[:])
                    if pair % 4 == 3:
                        mm.then_inc(PT_full, 1)
            if valid(i, u, 2):
                pe.wait_ge(shifted, n + 1)
                scores(u + 2)
            if u % 2 == 0 and valid(i, u, -6):
                job = side_job(i, u, "PL")
                bank_free(pe, job)
                s = (u - 6) // 2 % 2
                pe.wait_ge(before_step, i * BODY + (u - 4))
                o = side[:, job.bank, 0:2 * E]
                pe.matmul(o, earlier[:], picked[:, s].rearrange("p t e -> p (t e)"), start=True, stop=False)
                pe.matmul(o, ones[:], before[:, s].rearrange("p t e -> p (t e)"), start=False, stop=True)\
                    .then_inc(side_full, 1)
            if prepares(i, u):
                q = u // TPB + 1
                for name in QUARTER[u % TPB]:
                    prepare(name, q % 2, side_job(i, u, name), i * BODY + (TPB * q + TPB), i * 64 + (64 * (q // 2) + 64))
            if valid(i, u, -2):
                job = side_job(i, u, "RT")
                bank_free(pe, job)
                unloaded(pe, side_job(i, u - 1, "XT"))
                for k in range(KD):
                    mm = pe.matmul(side[:, job.bank, 0:E], xn2T[:, u % 2, k, :], gate[:, k, :],
                                   start=(k == 0), stop=(k == KD - 1))
                mm.then_inc(side_full, 1)
            if valid(i, u, 0):
                job = side_job(i, u, "O")
                bank_free(pe, job)
                pe.wait_ge(probsT_ready, n * 2 + 2)
                for pair in range(PAIRS):
                    mm = pe.matmul(side[:, job.bank, 0:D], probsT[:, u % 2, pair, :], U[:, u // TPB % 2, pair, :],
                                   start=(pair == 0), stop=(pair == PAIRS - 1))
                mm.then_inc(side_full, 1)
            if valid(i, u, -1):
                job = side_job(i, u, "XT")
                bank_free(pe, job)
                pe.wait_ge(xn2_ready, n)
                for k in range(KD):
                    mm = pe.transpose(side[:, job.bank, k * P:k * P + P], rows[:, (u - 1) % BODY, k * P:k * P + P], ident[:])
                mm.then_inc(side_full, 1)

        turns(pe, BODY, TURNS, DRAIN, step)

    @block.scalar
    def _(act):
        for j in range(4 * PAIRS):
            act.wait_ge(proj_full, j + 1)
            if j >= 4:
                act.wait_ge(kv_stored[j % 4], 16 * (j // 4))
            act.mul(kv_stage[:, j % 4], S[:, j // 2 % 2, j % 2 * N:j % 2 * N + N],
                    SCALE if j < 2 * PAIRS else 1.0).then_inc(proj_read, 1)

        def unload(name, s, job):
            j, o = int(name[1]), side[:, job.bank]
            act.wait_ge(side_full, job.count)
            if name[0] == "T":
                act.copy(xnT[:, s, j, :], o).then_inc(side_read[job.bank], 1)
            elif name[0] == "G":
                k, half = j // 2, j % 2
                act.copy(G[:, s, k, half * N:half * N + N], o).then_inc(side_read[job.bank], 1)
            else:
                act.copy(U[:, s, 2 * j:2 * j + 2, :], o.rearrange("p (q d) -> p q d", q=2))\
                   .then_inc(side_read[job.bank], 1)

        def exponentials(u, tiles):
            act.wait_ge(shifted, tiles)
            act.activation(probs[:, u % 2], probs[:, u % 2], ACT.Exp).then_inc(exp_done, 1)

        for name in PREP_ORDER:
            unload(name, 0, prep_job(0, 0, name))
        exponentials(0, 1)

        def step(i, u):
            n = i * BODY + u
            if valid(i, u, 0):
                for half in range(2):
                    act.wait_ge(PT_full, n * 2 + (half + 1))
                    pairs = slice(half * PAIRS // 2, (half + 1) * PAIRS // 2)
                    act.copy(probsT[:, u % 2, pairs], PT[:, pairs]).then_inc(probsT_ready, 1)
            if valid(i, u, 1):
                exponentials(u + 1, n + 2)
            if prepares(i, u):
                for name in QUARTER[u % TPB]:
                    unload(name, (u // TPB + 1) % 2, side_job(i, u, name))
            if valid(i, u, -2):
                job = side_job(i, u, "RT")
                act.wait_ge(side_full, job.count)
                act.activation(explog[:, (u - 2) // 2 % 2, u % 2], side[:, job.bank, 0:E], ACT.Exp, scale=-1.0)\
                   .then_inc(side_read[job.bank], 1)
            if valid(i, u, -1):
                job = side_job(i, u, "XT")
                act.wait_ge(side_full, job.count)
                act.copy(xn2T[:, (u - 1) % 2], side[:, job.bank, 0:D].rearrange("p (k t) -> p k t", k=KD))\
                   .then_inc(side_read[job.bank], 1)

        turns(act, BODY, TURNS, DRAIN, step)

    @block.gpsimd
    def _(pool):
        def pool_wait(signal, value):
            pool.wait_ge(signal, value)
            pool.tensor_tensor(waited_pool[:], eps[:, 0:1], eps[:, 0:1], ALU.add)

        pool.memset(kbd[:], 0.0)
        pool.memset(vbd[:], 0.0).then_inc(bd_zero, 1)
        pool.memset(minus_half[:], -0.5)
        pool.memset(eps[:], EPS)
        pool.memset(ones[:], 1.0)
        pool.memset(before[:, 1], 0.0)
        pool.memset(picked[:, 1], 0.0)
        pool.memset(rows[:, :, CW + E], 1.0)
        pool.memset(counts[:, E:EA], float(TILES))
        pool.memset(zeros[:], 0.0).then_inc(zeros_set, 1)
        pool.iota(rows[:, :, ID].bitcast(I32), pattern=[[P, BODY]], base=-TOK_PER_TURN, channel_multiplier=1)
        for t in range(2):
            pool.iota(first_row_i[:, t], pattern=[[ROOM, E]], base=1, channel_multiplier=0).then_inc(iota_set, 1)
        pool.iota(turn_i[:], pattern=[[0, 1]], base=TOK_PER_TURN, channel_multiplier=0).then_inc(iota_set, 1)
        pool.wait_ge(zeros_set, 1)
        pool.wait_ge(iota_set, 3)
        pool.tensor_copy(first_row[:], first_row_i[:])
        pool.affine_select(out=earlier[:], in_=ones[:], compare_op=ALU.is_gt, fill=0.0, base=0,
                           pattern=[[1, P]], channel_multiplier=-1)
        pool.memset(ident[:], 0.0).then_inc(ident_zero, 1)
        pool.wait_ge(ident_zero, 1)
        pool.affine_select(out=ident[:], in_=ident[:], compare_op=ALU.not_equal, fill=1.0, base=0,
                           pattern=[[-1, P]], channel_multiplier=1).then_inc(consts_set, 1)

        def reciprocal_deviation(slot, norms, steps):
            pool.wait_ge(stats_ready, steps)
            pool.tensor_tensor(veps[:, slot, norms], mv[:, slot, norms, 1], eps[:, norms], ALU.add).then_inc(veps_ready, 1)
            pool.wait_ge(veps_ready, steps)
            pool.tensor_tensor(rstd[:, slot, norms], veps[:, slot, norms], minus_half[:, norms], ALU.pow)\
                .then_inc(rstd_ready, 1)

        def residual(u, loads):
            pool.wait_ge(xres_in[u % 2], loads)
            pool.tensor_tensor(xres[:, u % 2], xres[:, u % 2], bo_b[:], ALU.add).then_inc(residual_ready, 1)

        for m in range(8):
            reciprocal_deviation(m % 2, slice(1, 2), m + 1)
        pool.wait_ge(consts_in, CONSTS)
        residual(0, 16)

        def step(i, u):
            n = i * BODY + u
            norms = slice(0 if valid(i, u, -1) else 1, 2 if valid(i, u, 8) else 1)
            if norms.start < norms.stop:
                reciprocal_deviation(u % 2, norms, n + 9)
            if u % 2 and valid(i, u, -5):
                s = (u - 5) // 2 % 2
                pool.wait_ge(routed, i * (BODY // 2) + (u - 3) // 2)
                if valid(i, u, -9):
                    unloaded(pool, side_job(i, u - 3, "PL"))
                pool.tensor_tensor(before[:, s, 0], before[:, 1 - s, 1], picked[:, 1 - s, 1], ALU.add).then_inc(before_step, 1)
                pool.wait_ge(before_step, i * BODY + (u - 4))
                pool.tensor_tensor(before[:, s, 1], before[:, s, 0], picked[:, s, 0], ALU.add).then_inc(before_step, 1)
            if valid(i, u, 1):
                residual(u + 1, i * (8 * BODY) + 16 * ((u + 1) // 2 + 1))
            if valid(i, u, -6):
                m, s, t = (u - 6) % BODY, (u - 6) // 2 % 2, u % 2
                if t == 0:
                    pool.wait_ge(slots_ready, i * (BODY // 2) + (u - 4) // 2)
                pool.tensor_tensor(rows[:, m, ID:ID + 1].bitcast(I32), rows[:, m, ID:ID + 1].bitcast(I32), turn_i[:], ALU.add)\
                    .then_inc(numbered, 1)
                pool_wait(numbered, i * BODY + (u - 5))
                for k in range(TOPK):
                    pool.indirect_dma_start(queue_d, bass.IndirectOffsetOnAxis(ap=slots[:, s, t, k:k + 1], axis=0),
                                            rows[:, m], None).then_inc(queued[m], 16)

        turns(pool, BODY, TURNS, DRAIN, step)
        pool.tensor_tensor(counts[:, 0:E], before[:, 1, 1], picked[:, 1, 1], ALU.add).then_inc(counted, 1)
        for m in range(BODY):
            pool.wait_ge(queued[m], 16 * TOPK * TURNS)
        pool.wait_ge(counted, 1)

    @block.vector
    def _(dve):
        def wait_on_copy(sem, value, of):
            dve.wait_ge(sem, value)
            dve.tensor_copy(waited[:, 0:of.shape[1]], of)

        def first_stats(u, loads):
            dve.wait_ge(xin_in[u % 4], loads)
            return dve.bn_stats(bn[:, u % 2, 1], xin[:, u % 4])

        def normalise(to, of, slot, norm):
            return dve.tensor_scalar(to, of, mv[:, slot, norm, 0:1], rstd[:, slot, norm:norm + 1], ALU.subtract, ALU.mult)

        def shift(u, tiles):
            scores = S[:, u % 2].rearrange("p (h c) -> p h c", c=C)
            dve.wait_ge(S_full, tiles)
            dve.tensor_reduce(rowmax[:, u % 2], scores, AX.X, ALU.max).then_inc(max_ready, 1)
            dve.wait_ge(max_ready, tiles)
            dve.tensor_tensor(probs[:, u % 2].rearrange("p (h c) -> p h c", c=C), scores,
                              rowmax[:, u % 2].unsqueeze(2).to_broadcast([P, H, C]), ALU.subtract).then_inc(shifted, 1)

        def divide(u, tiles):
            p = probs[:, u % 2].rearrange("p (h c) -> p h c", c=C)
            dve.wait_ge(exp_done, tiles)
            dve.tensor_reduce(rowsum[:, u % 2], p, AX.X, ALU.add).then_inc(sum_ready, 1)
            dve.wait_ge(sum_ready, tiles)
            dve.reciprocal(rowinv[:, u % 2], rowsum[:, u % 2]).then_inc(inv_ready, 1)
            dve.wait_ge(inv_ready, tiles)
            dve.tensor_tensor(p, p, rowinv[:, u % 2].unsqueeze(2).to_broadcast([P, H, C]), ALU.mult)\
               .then_inc(probs_ready, 1)

        for m in range(8):
            first_stats(m, 16 * (m // 4 + 1)).then_inc(bn_done, 1)
            dve.wait_ge(bn_done, m + 1)
            dve.bn_aggr(mv[:, m % 2, 1], bn[:, m % 2, 1]).then_inc(stats_ready, 1)
            dve.wait_ge(rstd_ready, m + 1)
            normalise(xn[:, m // TPB, m % TPB], xin[:, m % 4], m % 2, 1).then_inc(xn_ready, 1)
        dve.wait_ge(consts_in, CONSTS)
        shift(0, 1)
        divide(0, 1)

        def route(i, u, c):
            s = (u - 4) // 2 % 2
            unloaded(dve, side_job(i, u - 1, "RT"))
            dve.tensor_scalar(denom[:], explog[:, s], 1.0, None, ALU.add).then_inc(scored, 1)
            dve.wait_ge(scored, c * 2 + 1)
            dve.reciprocal(score[:], denom[:]).then_inc(scored, 1)
            dve.wait_ge(scored, c * 2 + 2)
            dve.tensor_tensor(biased[:], score[:], gb_b[:], ALU.add).then_inc(biased_ready, 1)
            wait_on_copy(biased_ready, c + 1, biased[:, 0:1, 0:1])
            for t in range(2):
                top = dve.max(top8[:, t], biased[:, t])
            top.then_inc(top_ready, 1)
            dve.wait_ge(top_ready, c * 2 + 1)
            dve.memset(top8[:, :, TOPK:8], NEVER).then_inc(top_ready, 1)
            wait_on_copy(top_ready, c * 2 + 2, top8[:, 0:1, 0:1])
            for t in range(2):
                top = dve.match_replace(rest[:, t], top8[:, t], biased[:, t], -NEVER)
            top.then_inc(picked_ready, 1)
            dve.wait_ge(picked_ready, c * 2 + 1)
            dve.tensor_tensor(picked[:, s], rest[:], biased[:], ALU.not_equal).then_inc(picked_ready, 1)
            dve.wait_ge(picked_ready, c * 2 + 2)
            dve.tensor_tensor(weight[:], picked[:, s], score[:], ALU.mult).then_inc(weight_ready, 1)
            dve.wait_ge(weight_ready, c + 1)
            dve.tensor_reduce(wsum[:], weight[:], AX.X, ALU.add).then_inc(wsum_ready, 1)
            dve.wait_ge(wsum_ready, c * 2 + 1)
            dve.reciprocal(winv[:], wsum[:]).then_inc(wsum_ready, 1)
            dve.wait_ge(wsum_ready, c * 2 + 2)
            m = (u - 4) % BODY
            dve.scalar_tensor_tensor(out=rows[:, m:m + 2, CW:CW + E], in0=weight[:], scalar=ROUTE_SCALE,
                                     in1=winv[:].unsqueeze(2).to_broadcast([P, 2, E]), op0=ALU.mult, op1=ALU.mult)\
               .then_inc(routed, 1)

        def queue_slots(i, u, c):
            s = (u - 6) // 2 % 2
            job = side_job(i, u, "PL")
            dve.wait_ge(side_full, job.count)
            dve.tensor_tensor(place[:], side[:, job.bank, 0:2 * E].rearrange("p (t e) -> p t e", t=2), first_row[:],
                              ALU.add).then_inc(side_read[job.bank], 1)
            unloaded(dve, job)
            dve.tensor_tensor(placed[:], place[:], picked[:, s], ALU.mult).then_inc(place_step, 1)
            wait_on_copy(place_step, c * 2 + 1, placed[:, 0:1, 0:1])
            for t in range(2):
                top = dve.max(place8[:, t], placed[:, t])
            top.then_inc(place_step, 1)
            dve.wait_ge(place_step, c * 2 + 2)
            if valid(i, u, -9):
                dve.wait_ge(queued[(u - 9) % BODY], i * (16 * TOPK) + 16 * TOPK * ((u - 9) // BODY + 1))
            if valid(i, u, -10):
                dve.wait_ge(queued[(u - 10) % BODY], i * (16 * TOPK) + 16 * TOPK * ((u - 10) // BODY + 1))
            dve.tensor_scalar(slots[:, s], place8[:, :, 0:TOPK], -1.0, None, ALU.add).then_inc(slots_ready, 1)

        def step(i, u):
            n = i * BODY + u
            second, first = valid(i, u, -1), valid(i, u, 8)
            norms = slice(0 if second else 1, 2 if first else 1)
            if second:
                job = side_job(i, u - 1, "O")
                s = (u - 1) % 2
                dve.wait_ge(side_full, job.count)
                dve.wait_ge(residual_ready, n)
                if valid(i, u, -3):
                    dve.wait_ge(x1_stored[s], i * (8 * BODY) + 16 * ((u - 1) // 2))
                dve.tensor_tensor(x1[:, s], side[:, job.bank, 0:D], xres[:, s], ALU.add).then_inc(side_read[job.bank], 1)
                unloaded(dve, job)
                last = dve.bn_stats(bn[:, u % 2, 0], x1[:, s])
            if first:
                last = first_stats(u, i * 32 + 16 * (u // 4 + 3))
            if second or first:
                last.then_inc(bn_done, 1)
                wait_on_copy(bn_done, n + 9, bn[:, u % 2, norms, 0:1])
                if second:
                    last = dve.bn_aggr(mv[:, u % 2, 0], bn[:, u % 2, 0])
                if first:
                    last = dve.bn_aggr(mv[:, u % 2, 1], bn[:, u % 2, 1])
                last.then_inc(stats_ready, 1)
            if valid(i, u, 1):
                shift(u + 1, n + 2)
            if second or first:
                dve.wait_ge(rstd_ready, n + 9)
            if second:
                if valid(i, u, -9):
                    dve.wait_ge(queued[(u - 1) % BODY], i * (16 * TOPK) + 16 * TOPK * ((u - 9) // BODY + 1))
                    dve.wait_ge(shared_queued[(u - 1) % BODY], i * 16 + 16 * ((u - 9) // BODY + 1))
                normalise(rows[:, (u - 1) % BODY, 0:D], x1[:, (u - 1) % 2], u % 2, 0).then_inc(xn2_ready, 1)
            if first:
                normalise(xn[:, u // TPB % 2, u % TPB], xin[:, u % 4], u % 2, 1).then_inc(xn_ready, 1)
            if u % 2 == 0 and valid(i, u, -6):
                queue_slots(i, u, i * (BODY // 2) + (u - 6) // 2)
            if u % 2 == 0 and valid(i, u, -4):
                route(i, u, i * (BODY // 2) + (u - 4) // 2)
            if valid(i, u, 1):
                divide(u + 1, n + 2)

        turns(dve, BODY, TURNS, DRAIN, step)


def phase_t(nc, ctx, ident, ones, counts, scratch):
    queue_d, table_d, ends_d = (scratch[k] for k in ("queue", "table", "ends"))
    CHUNKS = 2

    def sb(name, shape, dt=F32):
        return ctx.enter_context(nc.sbuf_tensor(name, shape, dt))

    def sem(name):
        return ctx.enter_context(nc.semaphore(name))

    upto = sb("upto", [EA, 2, EA])
    number = sb("number", [P, CHUNKS])
    number_i = sb("number_i", [P, CHUNKS], I32)
    base = sb("base", [EA, 1])
    base_i = sb("base_i", [EA, 1], I32)
    padding = sb("padding", [P, STEP // P, ROW])
    n_s = sb("n_s", [EA, P])
    guess = sb("guess", [EA, P])
    guess_i = sb("guess_i", [EA, P], I32)
    guessed = sb("guessed", [EA, P])
    short = sb("short", [EA, P])
    blocks = sb("blocks", [EA, P])
    cum = sb("cum", [P, 2, EA])
    gone = sb("gone", [P, 2, CHUNKS, EA])
    sums = sb("gone_sums", [P, 2, CHUNKS])
    within = sb("within", [P, CHUNKS])
    used = sb("used", [P, CHUNKS])
    offset = sb("offset", [P, CHUNKS])
    masked = sb("masked", [P, CHUNKS])
    table = sb("table", [P, 3, CHUNKS], I32)
    waits = sb("waits", [P, CHUNKS])
    waits_i = sb("waits_i", [P, CHUNKS], I32)
    opening = sb("opening", [P, CHUNKS])
    ends_i = sb("ends_i", [EA, 1], I32)
    ends_row = sb("ends_row", [1, EA], I32)
    N_PS = ctx.enter_context(nc.psum_tensor("N_PS", [EA, P], F32))
    CUM = ctx.enter_context(nc.psum_tensor("CUM", [P, 2 * EA], F32))

    numbers_set = sem("numbers_set")
    t_consts = sem("t_consts")
    n_full = sem("n_full")
    made = sem("made")
    blocks_ready = sem("blocks_ready")
    cum_full = sem("cum_full")
    table_ready = sem("table_ready")
    ends_ready = sem("ends_ready")
    table_stored = sem("table_stored")
    ends_stored = sem("ends_stored")
    ends_in = sem("ends_in")
    padded = sem("padded")
    block = ctx.enter_context(nc.Block())

    @block.gpsimd
    def _(pool):
        def pool_wait(signal, value):
            pool.wait_ge(signal, value)
            pool.tensor_tensor(waited_pool[:], eps[:, 0:1], eps[:, 0:1], ALU.add)

        pool.iota(number_i[:], pattern=[[1, CHUNKS]], base=0, channel_multiplier=CHUNKS).then_inc(numbers_set, 1)
        pool.iota(waits_i[:], pattern=[[32, CHUNKS]], base=-32, channel_multiplier=32).then_inc(numbers_set, 1)
        pool.iota(base_i[:], pattern=[[0, 1]], base=0, channel_multiplier=ROOM).then_inc(numbers_set, 1)
        pool.memset(padding[:], 0.0).then_inc(numbers_set, 1)
        pool.wait_ge(numbers_set, 4)
        pool.tensor_copy(waits[:], waits_i[:])
        pool.tensor_copy(number[:], number_i[:])
        pool.tensor_copy(base[:], base_i[:])
        pool.tensor_copy(upto[:, 1], ident[0:EA, 0:EA])
        pool.affine_select(out=upto[:, 0], in_=ones[0:EA, 0:EA], compare_op=ALU.is_ge, fill=0.0, base=0,
                           pattern=[[1, EA]], channel_multiplier=-1)
        pool.iota(padding[:, :, ID].bitcast(I32), pattern=[[P, STEP // P]], base=TOK, channel_multiplier=1)\
            .then_inc(t_consts, 1)

    @block.tensor
    def _(pe):
        pe.matmul(N_PS[:], counts[:], ones[:], start=True, stop=True).then_inc(n_full, 1)
        pe.wait_ge(t_consts, 1)
        pe.wait_ge(blocks_ready, 1)
        pe.matmul(CUM[:], blocks[:], upto[:].rearrange("p a e -> p (a e)"), start=True, stop=True).then_inc(cum_full, 1)

    @block.vector
    def _(dve):
        steps = [0]

        def then(instruction):
            steps[0] += 1
            instruction.then_inc(made, 1)
            dve.wait_ge(made, steps[0])

        dve.wait_ge(t_consts, 1)
        dve.wait_ge(n_full, 1)
        then(dve.tensor_copy(n_s[:], N_PS[:]))
        dve.tensor_tensor(ends_i[:], n_s[:, 0:1], base[:], ALU.add).then_inc(ends_ready, 1)
        then(dve.tensor_scalar(guess[:], n_s[:], 1.0 / STEP, 0.5 - 0.5 / STEP, ALU.mult, ALU.add))
        then(dve.tensor_copy(guess_i[:], guess[:]))
        then(dve.tensor_copy(guessed[:], guess_i[:]))
        then(dve.scalar_tensor_tensor(out=short[:], in0=guessed[:], scalar=float(STEP), in1=n_s[:], op0=ALU.mult, op1=ALU.is_lt))
        dve.tensor_tensor(blocks[:], guessed[:], short[:], ALU.add).then_inc(blocks_ready, 1)
        dve.wait_ge(cum_full, 1)
        then(dve.tensor_copy(cum[:], CUM[:].rearrange("p (a e) -> p a e", a=2)))
        for c in range(CHUNKS):
            last = dve.tensor_scalar(gone[:, 0, c], cum[:, 0], number[:, c:c + 1], None, ALU.is_le)
        then(last)
        then(dve.tensor_tensor(gone[:, 1], gone[:, 0], cum[:, 1:2].to_broadcast([P, CHUNKS, EA]), ALU.mult))
        then(dve.tensor_reduce(sums[:], gone[:], AX.X, ALU.add))
        dve.tensor_scalar(used[:], sums[:, 0], EA - 0.5, None, ALU.is_lt)
        dve.tensor_scalar(offset[:], sums[:, 0], float(ROOM), None, ALU.mult)
        then(dve.tensor_tensor(within[:], number[:], sums[:, 1], ALU.subtract))
        then(dve.scalar_tensor_tensor(out=masked[:], in0=within[:], scalar=float(STEP), in1=used[:], op0=ALU.mult, op1=ALU.mult))
        then(dve.tensor_scalar(opening[:], masked[:], 0.0, None, ALU.is_equal))
        dve.scalar_tensor_tensor(out=table[:, 2], in0=opening[:], scalar=32.0, in1=waits[:], op0=ALU.mult, op1=ALU.add)
        dve.tensor_tensor(table[:, 0], masked[:], offset[:], ALU.add)
        dve.tensor_scalar(table[:, 1], sums[:, 0], float(EA - 1), None, ALU.min).then_inc(table_ready, 1)

    @block.sync
    def _(sp):
        sp.wait_ge(ends_ready, 1)
        sp.dma_start(ends_d, ends_i[:]).then_inc(ends_stored, 16)
        sp.wait_ge(ends_stored, 16)
        sp.dma_start(ends_row[:], ends_d.rearrange("e a -> a e", a=1)).then_inc(ends_in, 16)
        sp.wait_ge(t_consts, 1)
        sp.dma_start(queue_d[EA * ROOM:].rearrange("(t p) d -> p t d", p=P), padding[:]).then_inc(padded, 16)
        sp.wait_ge(ends_in, 16)
        for e in range(EA):
            end = sp.value_load(ends_row[0:1, e:e + 1], min_val=0, max_val=EA * ROOM)
            sp.dma_start(queue_d[bass.ds(end, STEP)].rearrange("(t p) d -> p t d", p=P), padding[:]).then_inc(padded, 16)
        sp.wait_ge(table_ready, 1)
        for a in range(3):
            sp.dma_start(table_d[a].rearrange("(p c) -> p c", c=CHUNKS), table[:, a]).then_inc(table_stored, 16)
        sp.wait_ge(table_stored, 48)
        sp.wait_ge(padded, 16 * (EA + 1))


E_TURNS = STEPS // E_BODY
HALVES = STEP // P


def phase_e(nc, ctx, w13, w2, w13_s, w2_s, ident, scratch, out_sums):
    queue_d, table_d = scratch["queue"], scratch["table"]

    def sb(name, shape, dt=F32):
        return ctx.enter_context(nc.sbuf_tensor(name, shape, dt))

    def sem(name):
        return ctx.enter_context(nc.semaphore(name))

    w13_hl = sb("w13_hl", [P, EA, KD, 2, 2 * I], F32R)
    w2_hl = sb("w2_hl", [P, EA, 2, D], F32R)
    stage = sb("stage", [P, 2, 3, D])
    steps_t = sb("steps_t", [1, 6 * P], I32)
    X = sb("X", [P, E_BODY, HALVES, ROW])
    xT_hl = sb("xT_hl", [P, 2, 2, KD, STEP], F32R)
    gated = sb("gated", [P, 2, HALVES, I])
    hid = sb("hid", [P, 2, HALVES, I])
    hidT_hl = sb("hidT_hl", [P, 2, 2, STEP], F32R)
    y = sb("y", [P, 4, HALVES, D])
    waited_e = sb("waited_e", [P, 2])
    XT = ctx.enter_context(nc.psum_tensor("XT", [P, 2, KD, STEP], F32))
    UP = ctx.enter_context(nc.psum_tensor("UP", [P, 2, HALVES, 2 * I], F32))
    HT = ctx.enter_context(nc.psum_tensor("HT", [P, 2, 2 * STEP], F32))
    Y = ctx.enter_context(nc.psum_tensor("Y", [P, 2, HALVES, D], F32))

    steps_in = sem("steps_in")
    stage_in = [sem("stage_in0"), sem("stage_in1")]
    w_high = sem("w_high")
    w_low = sem("w_low")
    waited_set = sem("waited_set")
    may_add = sem("may_add")
    rows_in = [sem(f"rows_in{i}") for i in range(E_BODY)]
    xt_full = sem("xt_full")
    x_high = sem("x_high")
    x_low = sem("x_low")
    up_full = sem("up_full")
    gated_ready = sem("gated_ready")
    hid_ready = sem("hid_ready")
    ht_full = sem("ht_full")
    ht_high = sem("ht_high")
    ht_low = sem("ht_low")
    y_full = sem("y_full")
    y_ready = sem("y_ready")
    added = [sem("added0"), sem("added1")]
    block = ctx.enter_context(nc.Block())

    def ok(i, u, d):
        return 0 <= i * E_BODY + u + d < STEPS if isinstance(i, int) else True

    def loads(i, u):
        return i * 16 + 16 * (u // E_BODY + 1)

    def adds(i, u):
        return i * (16 * E_BODY) + 32 * (u // 2 + 1)

    def first_row(i, u):
        m = i * E_BODY + u
        return steps_t[0:1, bass.ds(m, 1)]

    def expert(i, u):
        m = i * E_BODY + (2 * P + u)
        return steps_t[0:1, bass.ds(m, 1)]

    def order(i, u):
        m = i * E_BODY + (4 * P + u)
        return steps_t[0:1, bass.ds(m, 1)]

    AHEAD = 4

    @block.sync
    def _(sp):
        sp.dma_start(steps_t[:], table_d.rearrange("a n -> (a n)").rearrange("(o n) -> o n", o=1)).then_inc(steps_in, 16)
        for e in range(EA):
            s = e % 2
            if e >= 2:
                sp.wait_ge(w_low, 2 * e - 2)
            a, b = (w13[:, e], w2[:, e]) if e < E else (w13_s, w2_s)
            sp.dma_start(stage[:, s, 0:KD], a.rearrange("(k p) n -> p k n", p=P)).then_inc(stage_in[s], 16)
            sp.dma_start(stage[:, s, KD], b).then_inc(stage_in[s], 16)
        sp.wait_ge(steps_in, 16)

        def load(i, u):
            row = sp.value_load(first_row(i, u), min_val=0, max_val=EA * ROOM)
            if ok(i, u, -E_BODY):
                sp.wait_ge(added[u % 2], adds(i, u - E_BODY))
            sp.dma_start(X[:, u % E_BODY], queue_d[bass.ds(row, STEP)].rearrange("(t p) d -> p t d", p=P))\
                .then_inc(rows_in[u % E_BODY], 16)

        for u in range(AHEAD):
            load(0, u)

        def step(i, u):
            if ok(i, u, AHEAD):
                load(i, u + AHEAD)

        turns(sp, E_BODY, E_TURNS, 0, step)

    @block.tensor
    def _(pe):
        pe.wait_ge(steps_in, 16)
        pe.wait_ge(w_high, 2 * EA)
        pe.wait_ge(w_low, 2 * EA)

        def transposes(i, u):
            m = i * E_BODY + u
            if ok(i, u, -2):
                pe.wait_ge(x_low, m - 1)
            pe.wait_ge(rows_in[u % E_BODY], loads(i, u))
            for k in range(KD):
                for t in range(HALVES):
                    mm = pe.transpose(XT[:, u % 2, k, t * P:t * P + P], X[:, u % E_BODY, t, k * P:k * P + P], ident[:])
            mm.then_inc(xt_full, 1)

        transposes(0, 0)

        def step(i, u):
            m = i * E_BODY + u
            if ok(i, u, 0):
                e = pe.value_load(expert(i, u), min_val=0, max_val=EA - 1)
                if ok(i, u, -2):
                    pe.wait_ge(hid_ready, m - 1)
                pe.wait_ge(x_low, m + 1)
                passes = [(xh, wh, k) for xh, wh in ((0, 0), (0, 1), (1, 0)) for k in range(KD)]
                for t in range(HALVES):
                    for xh, wh, k in passes:
                        mm = pe.matmul(UP[:, u % 2, t], xT_hl[:, u % 2, xh, k, t * P:t * P + P],
                                       w13_hl[:, bass.ds(e, 1), k, wh, :].rearrange("p a n -> p (a n)"),
                                       start=((xh, wh, k) == passes[0]), stop=((xh, wh, k) == passes[-1]))
                mm.then_inc(up_full, 1)
            if ok(i, u, 1):
                transposes(i, u + 1)
            if ok(i, u, -1):
                if ok(i, u, -3):
                    pe.wait_ge(ht_low, m - 2)
                pe.wait_ge(hid_ready, m)
                for t in range(HALVES):
                    mm = pe.transpose(HT[:, (u - 1) % 2, t * P:t * P + P], hid[:, (u - 1) % 2, t], ident[:])
                mm.then_inc(ht_full, 1)
            if ok(i, u, -2):
                e = pe.value_load(expert(i, u - 2), min_val=0, max_val=EA - 1)
                if ok(i, u, -4):
                    pe.wait_ge(y_ready, m - 3)
                pe.wait_ge(ht_low, m - 1)
                for t in range(HALVES):
                    for hh, wh in ((0, 0), (0, 1), (1, 0)):
                        mm = pe.matmul(Y[:, u % 2, t], hidT_hl[:, u % 2, hh, t * P:t * P + P],
                                       w2_hl[:, bass.ds(e, 1), wh, :].rearrange("p a d -> p (a d)"),
                                       start=(hh + wh == 0), stop=(hh == 1))
                mm.then_inc(y_full, 1)

        turns(pe, E_BODY, E_TURNS, 3, step)

    @block.scalar
    def _(act):
        for e in range(EA):
            s = e % 2
            act.wait_ge(stage_in[s], 32 * (e // 2 + 1))
            act.copy(w13_hl[:, e, :, 0], stage[:, s, 0:KD]).then_inc(w_high, 1)
            act.copy(w2_hl[:, e, 0], stage[:, s, KD]).then_inc(w_high, 1)

        def x_highs(i, u):
            m = i * E_BODY + u
            act.wait_ge(xt_full, m + 1)
            if ok(i, u, -2):
                act.wait_ge(up_full, m - 1)
            act.copy(xT_hl[:, u % 2, 0], XT[:, u % 2]).then_inc(x_high, 1)

        x_highs(0, 0)

        def step(i, u):
            m = i * E_BODY + u
            if ok(i, u, 0):
                act.wait_ge(up_full, m + 1)
                if ok(i, u, -2):
                    act.wait_ge(hid_ready, m - 1)
                act.activation(gated[:, u % 2], UP[:, u % 2, :, 0:I], ACT.Silu).then_inc(gated_ready, 1)
            if ok(i, u, 1):
                x_highs(i, u + 1)
            if ok(i, u, -1):
                act.wait_ge(ht_full, m)
                if ok(i, u, -3):
                    act.wait_ge(y_full, m - 2)
                act.copy(hidT_hl[:, (u - 1) % 2, 0], HT[:, (u - 1) % 2, 0:STEP]).then_inc(ht_high, 1)
            if ok(i, u, -2):
                act.wait_ge(y_full, m - 1)
                if ok(i, u, -6):
                    act.wait_ge(added[u % 2], adds(i, u - 6))
                act.copy(y[:, (u - 2) % 4], Y[:, u % 2]).then_inc(y_ready, 1)

        turns(act, E_BODY, E_TURNS, 3, step)

    @block.vector
    def _(dve):
        for e in range(EA):
            s = e % 2
            dve.wait_ge(w_high, 2 * e + 2)
            dve.tensor_tensor(w13_hl[:, e, :, 1], stage[:, s, 0:KD], w13_hl[:, e, :, 0].bitcast(F32), ALU.subtract)\
               .then_inc(w_low, 1)
            dve.tensor_tensor(w2_hl[:, e, 1], stage[:, s, KD], w2_hl[:, e, 0].bitcast(F32), ALU.subtract).then_inc(w_low, 1)
        dve.wait_ge(steps_in, 16)

        def x_lows(i, u):
            m = i * E_BODY + u
            dve.wait_ge(x_high, m + 1)
            dve.tensor_tensor(xT_hl[:, u % 2, 1], XT[:, u % 2], xT_hl[:, u % 2, 0].bitcast(F32), ALU.subtract).then_inc(x_low, 1)

        x_lows(0, 0)

        def step(i, u):
            m = i * E_BODY + u
            if ok(i, u, 0):
                e = dve.value_load(expert(i, u), min_val=0, max_val=EA - 1)
                if ok(i, u, -2):
                    dve.wait_ge(ht_full, m - 1)
                dve.wait_ge(gated_ready, m + 1)
                for t in range(HALVES):
                    last = dve.scalar_tensor_tensor(out=hid[:, u % 2, t], in0=UP[:, u % 2, t, I:2 * I],
                                                    scalar=X[:, u % E_BODY, t, bass.ds(e + CW, 1)],
                                                    in1=gated[:, u % 2, t], op0=ALU.mult, op1=ALU.mult)
                last.then_inc(hid_ready, 1)
            if ok(i, u, 1):
                x_lows(i, u + 1)
            if ok(i, u, -1):
                dve.wait_ge(ht_high, m)
                dve.tensor_tensor(hidT_hl[:, (u - 1) % 2, 1], HT[:, (u - 1) % 2, 0:STEP],
                                  hidT_hl[:, (u - 1) % 2, 0].bitcast(F32), ALU.subtract).then_inc(ht_low, 1)

        turns(dve, E_BODY, E_TURNS, 3, step)

    @block.gpsimd
    def _(pool):
        def pool_wait(signal, value):
            pool.wait_ge(signal, value)
            pool.tensor_tensor(waited_pool[:], eps[:, 0:1], eps[:, 0:1], ALU.add)

        pool.memset(waited_e[:], 0.0).then_inc(waited_set, 1)
        pool.wait_ge(steps_in, 16)
        pool.wait_ge(waited_set, 1)

        def step(i, u):
            m = i * E_BODY + u
            pool.wait_ge(y_ready, m + 1)
            if ok(i, u, -1):
                if isinstance(i, int) and i * E_BODY + u < 3:
                    pool.wait_ge(added[(u - 1) % 2], adds(i, u - 1))
                else:
                    before = pool.value_load(order(i, u), min_val=32, max_val=16 * STEPS + 32)
                    pool.wait_ge(added[(u - 1) % 2], before)
            if ok(i, u, -2):
                pool.wait_ge(added[u % 2], adds(i, u - 2))
            if ok(i, u, -1):
                pool.wait_ge(may_add, m)
            pool.tensor_tensor(waited_e[:, 0:1], waited_e[:, 1:2], waited_e[:, 1:2], ALU.add).then_inc(may_add, 1)
            for t in range(HALVES):
                pool.indirect_dma_start(out_sums, bass.IndirectOffsetOnAxis(ap=X[:, u % E_BODY, t, ID:ID + 1].bitcast(U32), axis=0),
                                        y[:, u % 4, t], None, compute_op=ALU.add).then_inc(added[u % 2], 16)

        turns(pool, E_BODY, E_TURNS, 0, step)
        for s in range(2):
            pool.wait_ge(added[s], 16 * STEPS)


def kernel(**inputs):
    import numpy as np
    import concourse.bacc as bacc
    from concourse.bass_utils import run_bass_kernel_spmd

    a = {k: np.asarray(v) for k, v in inputs.items()}
    arrays = {
        "x": a["x"],
        "ctxT": a["ctx_1024"].reshape(B * C, D).T,
        "wq": a["L0_xattn_Wq"].T,
        "wk": a["L0_xattn_Wk"],
        "wv": a["L0_xattn_Wv"],
        "wo": a["L0_xattn_Wo"],
        "bo": a["L0_xattn_bo"],
        "gateT": a["L0_ffn_gate_w"].T,
        "gate_b": a["L0_ffn_gate_b"],
        "w13": a["L0_ffn_w13"].transpose(2, 0, 1),
        "w2": a["L0_ffn_w2"].transpose(2, 0, 1),
        "w13_s": a["L0_ffn_w13_s"].T,
        "w2_s": a["L0_ffn_w2_s"].T,
    }
    nc = bacc.Bacc("TRN2", target_bir_lowering=False, num_devices=1)
    feeds, args = {}, {}
    for name, value in arrays.items():
        value = np.ascontiguousarray(value)
        feeds[f"in_{name}"] = value
        args[name] = nc.dram_tensor(f"in_{name}", value.shape, mybir.dt.from_np(value.dtype), kind="ExternalInput").ap()
    args["sums"] = nc.dram_tensor("out_y", (SUMS, D), F32, kind="ExternalOutput").ap()
    build(nc, **args)
    r = run_bass_kernel_spmd(nc, [feeds], core_ids=[0])
    return np.asarray(r.results[0]["out_y"])[:TOK].reshape(B, N, D)
```

```python
from contextlib import ExitStack

import concourse.bass as bass
from concourse import mybir

F32 = mybir.dt.float32
F32R = mybir.dt.float32r
I32 = mybir.dt.int32
U32 = mybir.dt.uint32
ALU = mybir.AluOpType
ACT = mybir.ActivationFunctionType
AX = mybir.AxisListType

P = 128
B, N, D = 16, 512, 256
H, DH = 16, 64
C = 64
KD = D // P
PAIRS = H // 2
HC = H * C
TILES = B * N // P
TPB = N // P
E, I, TOPK = 16, 128, 4
EA = E + 1
SCALE = DH ** -0.5
ROUTE_SCALE = 2.5
TOK = B * N
STEP = 2 * P
ROOM = TOK + STEP
ROW = D + 1 + EA
ID, CW = D, D + 1
E_BODY = 8
STEPS = (TOK * TOPK + E * (STEP - 1)) // STEP + TOK // STEP
STEPS += -STEPS % E_BODY
SUMS = TOK + STEP
EPS = 1e-5
BODY = 2 * TPB
DRAIN = 6
TURNS = TILES // BODY
NEVER = 3.0e38


def build(nc, x, ctxT, wq, wk, wv, wo, bo, gateT, gate_b, w13, w2, w13_s, w2_s, sums):
    x_t = x.rearrange("b (t p) d -> (b t) p d", p=P)
    scratch = {
        "k": nc.dram_tensor("keys_scratch", [B, P, PAIRS, C], F32).ap(),
        "v": nc.dram_tensor("values_scratch", [B, P, PAIRS, C], F32).ap(),
        "queue": nc.dram_tensor("queue_scratch", [EA * ROOM + STEP, ROW], F32).ap(),
        "table": nc.dram_tensor("table_scratch", [3, 2 * P], I32).ap(),
        "ends": nc.dram_tensor("ends_scratch", [EA, 1], I32).ap(),
    }
    with ExitStack() as outer:
        ident = outer.enter_context(nc.sbuf_tensor("ident", [P, P], F32))
        ones = outer.enter_context(nc.sbuf_tensor("ones", [P, P], F32))
        counts = outer.enter_context(nc.sbuf_tensor("counts", [P, EA], F32))
        with ExitStack() as ctx:
            phase_a(nc, ctx, x_t, ctxT, wq, wk, wv, wo, bo, gateT, gate_b, ident, ones, counts, scratch, sums)
        with ExitStack() as ctx:
            phase_e(nc, ctx, w13, w2, w13_s, w2_s, ident, ones, counts, scratch, sums)


def turns(eng, body, count, drain, step):
    for u in range(body):
        step(0, u)
    with eng.Fori(1, count - 1) as i:
        for u in range(body):
            step(i, u)
    for u in range(body):
        step(count - 1, u)
    for u in range(drain):
        step(count, u)


QUARTER = [["T0", "T1", "G0"], ["G1", "G2", "G3"], ["U0", "U1"], ["U2", "U3"]]
PREP_ORDER = [name for quarter in QUARTER for name in quarter]


def side_jobs(m):
    names = list(QUARTER[m % TPB]) if m + TPB - m % TPB < TILES else []
    names += [name for name, lag in (("RT", 2), ("XT", 1)) if 0 <= m - lag < TILES]
    names += ["PL"] if m % 2 == 0 and 0 <= m - 6 < TILES else []
    return names + (["O"] if m < TILES else [])


def jobs_before(m):
    return len(PREP_ORDER) + sum(len(side_jobs(w)) for w in range(m))


TOK_PER_TURN = BODY * P
PER_TURN = jobs_before(3 * BODY) - jobs_before(2 * BODY)


class Job:

    def __init__(self, turn, at):
        self.count, self.before, self.bank = turn * PER_TURN + (at + 1), turn * (PER_TURN // 2) + at // 2, at % 2
        self.first = isinstance(turn, int) and turn == 0 and at < 2


def side_job(i, u, name):
    if isinstance(i, int):
        m = i * BODY + u
        return Job(0, jobs_before(m) + side_jobs(m).index(name))
    m = 2 * BODY + u
    return Job(i, jobs_before(m) + side_jobs(m).index(name) - 2 * PER_TURN)


def prep_job(i, u, name):
    if isinstance(i, int) and i * BODY + u < TPB:
        return Job(0, PREP_ORDER.index(name))
    quarter = [name in q for q in QUARTER].index(True)
    return side_job(i, u // TPB * TPB - TPB + quarter, name)


PREP_PER_TURN = len(PREP_ORDER) * BODY // TPB


def prep_at(u, name):
    return len(PREP_ORDER) * (u // TPB + 1) + PREP_ORDER.index(name)


PASSES = ((0, 0), (0, 1), (1, 0))


def valid(i, u, d):
    return 0 <= i * BODY + u + d < TILES if isinstance(i, int) else True


def prepares(i, u):
    return not isinstance(i, int) or i * BODY + u + TPB - u % TPB < TILES


def after_first(i, u):
    return not isinstance(i, int) or i * BODY + u >= 1


def phase_a(nc, ctx, x_t, ctxT, wq, wk, wv, wo, bo, gateT, gate_b, ident, ones, counts, scratch, sums):
    k_d, v_d, queue_d = (scratch[k] for k in ("k", "v", "queue"))
    x1_d = sums[0:TOK].rearrange("(n p) d -> n p d", p=P)
    shared_d = queue_d[0:TOK].rearrange("(n p) d -> n p d", p=P)

    def sb(name, shape, dt=F32):
        return ctx.enter_context(nc.sbuf_tensor(name, shape, dt))

    def sem(name):
        return ctx.enter_context(nc.semaphore(name))

    bo_b = sb("bo_b", [P, D])
    gb_b = sb("gb_b", [P, 2, E])
    gate = sb("gate", [P, KD, E])
    minus_half = sb("minus_half", [P, 2])
    eps = sb("eps", [P, 2])
    waited_pool = sb("waited_pool", [P, 1])
    waited = sb("waited", [P, 2, 1])
    wqT = sb("wqT", [P, PAIRS, D])
    wo_s = sb("wo_s", [P, PAIRS, D])
    wk_s = sb("wk_s", [P, KD, H * DH])
    wv_s = sb("wv_s", [P, KD, H * DH])
    ctx_s = sb("ctx_s", [P, KD, B * C])
    staged = sb("staged", [P, 4, N])
    xin = sb("xin", [P, 4, D])
    xres = sb("xres", [P, 2, D])
    xn = sb("xn", [P, 2, TPB, D])
    xnT_hl = sb("xnT_hl", [P, 2, 2, KD, N], F32R)
    kbd = sb("kbd", [P, 2, PAIRS, P])
    vbd = sb("vbd", [P, 2, PAIRS, P])
    G_hl = sb("G_hl", [P, 2, 2, KD, HC], F32R)
    U_hl = sb("U_hl", [P, 2, 2, PAIRS, D], F32R)
    probs = sb("probs", [P, 2, HC])
    probsT_hl = sb("probsT_hl", [P, 2, 2, PAIRS, P], F32R)
    x1 = sb("x1", [P, 2, D])
    rows = sb("rows", [P, BODY, ROW])
    zeros = sb("zeros", [P, STEP // P, D])
    xn2T = sb("xn2T", [P, 2, KD, P])
    rowmax = sb("rowmax", [P, 2, H])
    rowneg = sb("rowneg", [P, 2, H])
    rowsum = sb("rowsum", [P, 2, H])
    rowinv = sb("rowinv", [P, 2, H])
    bn = sb("bn", [P, 2, 2, 6])
    mv = sb("mv", [P, 2, 2, 2])
    veps = sb("veps", [P, 2, 2])
    rstd = sb("rstd", [P, 2, 2])
    explog = sb("explog", [P, 2, 2, E])
    denom = sb("denom", [P, 2, E])
    score = sb("score", [P, 2, E])
    biased = sb("biased", [P, 2, E])
    top8 = sb("top8", [P, 2, 8])
    rest = sb("rest", [P, 2, E])
    picked = sb("picked", [P, 2, 2, E])
    before = sb("before", [P, 2, 2, E])
    weight = sb("weight", [P, 2, E])
    wsum = sb("wsum", [P, 2])
    winv = sb("winv", [P, 2])
    earlier = sb("earlier", [P, P])
    first_row_i = sb("first_row_i", [P, 2, E], I32)
    turn_i = sb("turn_i", [P, 1], I32)
    first_row = sb("first_row", [P, 2, E])
    place = sb("place", [P, 2, E])
    placed = sb("placed", [P, 2, E])
    place8 = sb("place8", [P, 2, 8])
    slots = sb("slots", [P, 2, 2, TOPK], U32)

    S = ctx.enter_context(nc.psum_tensor("S", [P, 2, HC], F32))
    PT = ctx.enter_context(nc.psum_tensor("PT", [P, PAIRS, P], F32))
    side = ctx.enter_context(nc.psum_tensor("side", [P, 2, N], F32))

    consts_in = sem("consts_in")
    wk_in = sem("wk_in")
    wv_in = sem("wv_in")
    proj_full = sem("proj_full")
    proj_read = sem("proj_read")
    kv_stored = [sem(f"kv_stored{i}") for i in range(4)]
    xin_in = [sem(f"xin_in{i}") for i in range(4)]
    xres_in = [sem(f"xres_in{i}") for i in range(2)]
    kv_in = [sem(f"kv_in{i}") for i in range(2)]
    x1_stored = [sem(f"x1_stored{i}") for i in range(2)]
    queued = [sem(f"queued{i}") for i in range(BODY)]
    shared_queued = [sem(f"shared_queued{i}") for i in range(BODY)]
    zeros_set = sem("zeros_set")
    iota_set = sem("iota_set")
    tail_zeroed = sem("tail_zeroed")
    before_step = sem("before_step")
    place_step = sem("place_step")
    slots_ready = sem("slots_ready")
    counted = sem("counted")
    numbered = sem("numbered")
    ident_zero = sem("ident_zero")
    bd_zero = sem("bd_zero")
    consts_set = sem("consts_set")
    bn_done = sem("bn_done")
    stats_ready = sem("stats_ready")
    veps_ready = sem("veps_ready")
    rstd_ready = sem("rstd_ready")
    xn_ready = sem("xn_ready")
    xn2_ready = sem("xn2_ready")
    S_full = sem("S_full")
    max_ready = sem("max_ready")
    maxima_ready = sem("maxima_ready")
    exp_done = sem("exp_done")
    inv_ready = sem("inv_ready")
    probs_ready = sem("probs_ready")
    residual_ready = sem("residual_ready")
    scored = sem("scored")
    biased_ready = sem("biased_ready")
    top_ready = sem("top_ready")
    picked_ready = sem("picked_ready")
    weight_ready = sem("weight_ready")
    wsum_ready = sem("wsum_ready")
    PT_full = sem("PT_full")
    probsT_high = sem("probsT_high")
    probsT_low = sem("probsT_low")
    split_high = sem("split_high")
    split_done = sem("split_done")
    side_full = sem("side_full")
    side_read = [sem("side_read0"), sem("side_read1")]
    routed = sem("routed")
    CONSTS = 16 * (4 + 2)

    block = ctx.enter_context(nc.Block())

    def unloaded(eng, job):
        eng.wait_ge(side_read[job.bank], job.before + 1)

    def bank_free(eng, job):
        if not job.first:
            eng.wait_ge(side_read[job.bank], job.before)

    @block.sync
    def _(sp):
        sp.dma_start(ctx_s[:], ctxT.rearrange("(k p) n -> p k n", p=P)).then_inc(wk_in, 16)
        sp.dma_start(wk_s[:], wk.rearrange("(k p) n -> p k n", p=P)).then_inc(wk_in, 16)
        sp.dma_start(wv_s[:], wv.rearrange("(k p) n -> p k n", p=P)).then_inc(wv_in, 16)
        for m in range(4):
            sp.dma_start(xin[:, m], x_t[m]).then_inc(xin_in[m], 16)
        sp.dma_start(wqT[:], wq.rearrange("(h p) n -> p h n", p=P)).then_inc(consts_in, 16)
        sp.dma_start(wo_s[:], wo.rearrange("(h p) n -> p h n", p=P)).then_inc(consts_in, 16)
        sp.dma_start(gate[:], gateT.rearrange("(k p) n -> p k n", p=P)).then_inc(consts_in, 16)
        sp.dma_start(bo_b[:], bo.rearrange("(a d) -> a d", a=1).to_broadcast([P, D])).then_inc(consts_in, 16)
        for t in range(2):
            sp.dma_start(gb_b[:, t], gate_b.rearrange("(a d) -> a d", a=1).to_broadcast([P, E])).then_inc(consts_in, 16)
        for m in range(4, 8):
            sp.wait_ge(xn_ready, m - 3)
            sp.dma_start(xin[:, m % 4], x_t[m]).then_inc(xin_in[m % 4], 16)
        for j in range(4 * PAIRS):
            to, pair, half = (k_d, v_d)[j // (2 * PAIRS)], j // 2 % PAIRS, j % 2
            sp.wait_ge(proj_read, j + 1)
            sp.dma_start(to[half * 8:half * 8 + 8, :, pair, :].rearrange("b p c -> p b c"),
                         staged[:, j % 4].rearrange("p (b c) -> p b c", c=C)).then_inc(kv_stored[j % 4], 16)
        for s in range(4):
            sp.wait_ge(kv_stored[s], 16 * PAIRS)

        def load_kv(b, s):
            for h in range(2):
                rows = slice(h * DH, h * DH + DH)
                sp.dma_start(kbd[rows, s, :, h * C:h * C + C], k_d[b, rows]).then_inc(kv_in[s], 16)
                sp.dma_start(vbd[rows, s, :, h * C:h * C + C], v_d[b, rows]).then_inc(kv_in[s], 16)

        sp.wait_ge(bd_zero, 1)
        load_kv(0, 0)
        load_kv(1, 1)
        sp.dma_start(xres[:, 0], x_t[0]).then_inc(xres_in[0], 16)

        def step(i, u):
            n = i * BODY + u
            if u % TPB == 0 and valid(i, u, 2 * TPB):
                b = i * 2 + u // TPB
                sp.wait_ge(side_full, prep_job(i, u, "U3").count)
                load_kv(b + 2, u // TPB)
            if valid(i, u, 8):
                sp.wait_ge(xn_ready, n + 5)
                sp.dma_start(xin[:, u % 4], x_t[n + 8]).then_inc(xin_in[u % 4], 16)
            if valid(i, u, 1):
                if after_first(i, u):
                    unloaded(sp, side_job(i, u - 1, "O"))
                sp.dma_start(xres[:, (u + 1) % 2], x_t[n + 1]).then_inc(xres_in[(u + 1) % 2], 16)
            if valid(i, u, -2):
                unloaded(sp, side_job(i, u - 2, "O"))
                sp.dma_start(x1_d[n - 2], x1[:, u % 2]).then_inc(x1_stored[u % 2], 16)
            if valid(i, u, -7):
                m = (u - 7) % BODY
                sp.wait_ge(numbered, i * BODY + (u - 6))
                sp.dma_start(shared_d[n - 7], rows[:, m]).then_inc(shared_queued[m], 16)

        sp.wait_ge(zeros_set, 1)
        sp.dma_start(sums[TOK:SUMS].rearrange("(t p) d -> p t d", p=P), zeros[:]).then_inc(tail_zeroed, 16)
        turns(sp, BODY, TURNS, DRAIN + 1, step)
        for s in range(2):
            sp.wait_ge(x1_stored[s], 16 * TILES // 2)
        sp.wait_ge(tail_zeroed, 16)
        for m in range(BODY):
            sp.wait_ge(shared_queued[m], 16 * TURNS)

    @block.tensor
    def _(pe):
        pe.wait_ge(wk_in, 32)
        for j in range(4 * PAIRS):
            w, pair, half = (wk_s, wv_s)[j // (2 * PAIRS)], j // 2 % PAIRS, j % 2
            if j == 2 * PAIRS:
                pe.wait_ge(wv_in, 16)
            if j >= 4:
                pe.wait_ge(proj_read, j - 3)
            for k in range(KD):
                mm = pe.matmul(S[:, j // 2 % 2, j % 2 * N:j % 2 * N + N], w[:, k, pair * P:pair * P + P],
                               ctx_s[:, k, half * N:half * N + N], start=(k == 0), stop=(k == KD - 1))
            mm.then_inc(proj_full, 1)
        pe.wait_ge(proj_read, 4 * PAIRS)
        pe.wait_ge(consts_in, CONSTS)
        pe.wait_ge(consts_set, 1)

        def prepare(name, s, job, tiles, loads):
            j, o = int(name[1]), side[:, job.bank]
            bank_free(pe, job)
            if name[0] == "T":
                pe.wait_ge(xn_ready, tiles)
                for t in range(TPB):
                    mm = pe.transpose(o[:, t * P:t * P + P], xn[:, s, t, j * P:j * P + P], ident[:])
            elif name[0] == "G":
                k, half = j // 2, j % 2
                pe.wait_ge(kv_in[s], loads)
                for q in range(PAIRS // 2):
                    pair = half * (PAIRS // 2) + q
                    mm = pe.matmul(o[:, q * P:q * P + P], wqT[:, pair, k * P:k * P + P], kbd[:, s, pair, :],
                                   start=True, stop=True)
            else:
                pe.wait_ge(kv_in[s], loads)
                for q in range(2):
                    mm = pe.matmul(o[:, q * D:q * D + D], vbd[:, s, 2 * j + q, :], wo_s[:, 2 * j + q, :],
                                   start=True, stop=True)
            mm.then_inc(side_full, 1)

        def scores(u):
            s, t = u // TPB % 2, u % TPB
            for half in range(2):
                passes = [(xh, gh, k) for xh, gh in PASSES for k in range(KD)]
                for xh, gh, k in passes:
                    mm = pe.matmul(S[:, u % 2, half * N:half * N + N], xnT_hl[:, s, xh, k, t * P:t * P + P],
                                   G_hl[:, s, gh, k, half * N:half * N + N],
                                   start=((xh, gh, k) == passes[0]), stop=((xh, gh, k) == passes[-1]))
            mm.then_inc(S_full, 1)

        for name in PREP_ORDER:
            prepare(name, 0, prep_job(0, 0, name), TPB, 64)
        pe.wait_ge(split_done, len(PREP_ORDER))
        scores(0)
        scores(1)

        def step(i, u):
            n = i * BODY + u
            if valid(i, u, 0):
                pe.wait_ge(probs_ready, n + 1)
                if after_first(i, u):
                    pe.wait_ge(probsT_low, n * 2)
                for pair in range(PAIRS):
                    mm = pe.transpose(PT[:, pair, :], probs[:, u % 2, pair * P:pair * P + P], ident[:])
                    if pair % 4 == 3:
                        mm.then_inc(PT_full, 1)
            if valid(i, u, 2):
                pe.wait_ge(exp_done, n + 1)
                if (u + 2) % TPB == 0:
                    pe.wait_ge(split_done, i * PREP_PER_TURN + (prep_at(u, "G3") + 1))
                scores(u + 2)
            if prepares(i, u):
                q = u // TPB + 1
                for name in QUARTER[u % TPB]:
                    prepare(name, q % 2, side_job(i, u, name), i * BODY + (TPB * q + TPB), i * 64 + (64 * (q // 2) + 64))
            if valid(i, u, -2):
                job = side_job(i, u, "RT")
                bank_free(pe, job)
                unloaded(pe, side_job(i, u - 1, "XT"))
                for k in range(KD):
                    mm = pe.matmul(side[:, job.bank, 0:E], xn2T[:, u % 2, k, :], gate[:, k, :],
                                   start=(k == 0), stop=(k == KD - 1))
                mm.then_inc(side_full, 1)
            if valid(i, u, -1):
                job = side_job(i, u, "XT")
                bank_free(pe, job)
                pe.wait_ge(xn2_ready, n)
                for k in range(KD):
                    mm = pe.transpose(side[:, job.bank, k * P:k * P + P], rows[:, (u - 1) % BODY, k * P:k * P + P], ident[:])
                mm.then_inc(side_full, 1)
            if u % 2 == 0 and valid(i, u, -6):
                job = side_job(i, u, "PL")
                bank_free(pe, job)
                s = (u - 6) // 2 % 2
                pe.wait_ge(before_step, i * BODY + (u - 4))
                o = side[:, job.bank, 0:2 * E]
                pe.matmul(o, earlier[:], picked[:, s].rearrange("p t e -> p (t e)"), start=True, stop=False)
                pe.matmul(o, ones[:], before[:, s].rearrange("p t e -> p (t e)"), start=False, stop=True)\
                    .then_inc(side_full, 1)
            if valid(i, u, 0):
                job = side_job(i, u, "O")
                bank_free(pe, job)
                if u % TPB == 0:
                    pe.wait_ge(split_done, i * PREP_PER_TURN + len(PREP_ORDER) * (u // TPB + 1))
                pe.wait_ge(probsT_low, n * 2 + 2)
                passes = [(ph, uh, pair) for ph, uh in PASSES for pair in range(PAIRS)]
                for ph, uh, pair in passes:
                    mm = pe.matmul(side[:, job.bank, 0:D], probsT_hl[:, u % 2, ph, pair, :], U_hl[:, u // TPB % 2, uh, pair, :],
                                   start=((ph, uh, pair) == passes[0]), stop=((ph, uh, pair) == passes[-1]))
                mm.then_inc(side_full, 1)

        turns(pe, BODY, TURNS, DRAIN, step)

    def prep_views(name, s, half):
        j = int(name[1])
        if name[0] == "T":
            return xnT_hl[:, s, half, j, :]
        if name[0] == "G":
            return G_hl[:, s, half, j // 2, j % 2 * N:j % 2 * N + N]
        return U_hl[:, s, half, 2 * j:2 * j + 2, :].rearrange("p q d -> p (q d)")

    @block.scalar
    def _(act):
        SPLITS = (9, 9, 9, 12)

        for j in range(4 * PAIRS):
            act.wait_ge(proj_full, j + 1)
            if j >= 4:
                act.wait_ge(kv_stored[j % 4], 16 * (j // 4))
            act.mul(staged[:, j % 4], S[:, j // 2 % 2, j % 2 * N:j % 2 * N + N],
                    SCALE if j < 2 * PAIRS else 1.0).then_inc(proj_read, 1)

        def unload(job, at, i=0):
            act.wait_ge(side_full, job.count)
            if not isinstance(i, int) or at >= 4:
                act.wait_ge(split_done, i * PREP_PER_TURN + (at - 3))
            act.copy(staged[:, at % 4], side[:, job.bank]).then_inc(side_read[job.bank], 1)

        def exponentials(u, tiles, heads):
            act.wait_ge(maxima_ready, tiles)
            for h in heads:
                last = act.activation(probs[:, u % 2, h * C:h * C + C], S[:, u % 2, h * C:h * C + C], ACT.Exp,
                                      bias=rowneg[:, u % 2, h:h + 1], accum_out=rowsum[:, u % 2, h:h + 1])
            if heads[-1] == H - 1:
                last.then_inc(exp_done, 1)

        for m in range(4):
            act.wait_ge(kv_stored[m], 16 * PAIRS)
        for at, name in enumerate(PREP_ORDER):
            unload(prep_job(0, 0, name), at)
        exponentials(0, 1, range(H))

        def step(i, u):
            n = i * BODY + u
            if valid(i, u, 0):
                for half in range(2):
                    act.wait_ge(PT_full, n * 2 + (half + 1))
                    pairs = slice(half * PAIRS // 2, (half + 1) * PAIRS // 2)
                    act.copy(probsT_hl[:, u % 2, 0, pairs], PT[:, pairs]).then_inc(probsT_high, 1)
            if valid(i, u, 1):
                exponentials(u + 1, n + 2, range(0, SPLITS[0]))
            names = QUARTER[u % TPB] if prepares(i, u) else []
            for j in range(3):
                if valid(i, u, 1) and SPLITS[j] < SPLITS[j + 1]:
                    exponentials(u + 1, n + 2, range(SPLITS[j], SPLITS[j + 1]))
                if j < len(names):
                    unload(side_job(i, u, names[j]), prep_at(u, names[j]), i)
            if valid(i, u, -2):
                job = side_job(i, u, "RT")
                act.wait_ge(side_full, job.count)
                if u % 2 == 0 and valid(i, u, -6):
                    act.wait_ge(routed, i * (BODY // 2) + (u - 4) // 2)
                act.activation(explog[:, (u - 2) // 2 % 2, u % 2], side[:, job.bank, 0:E], ACT.Exp, scale=-1.0)\
                   .then_inc(side_read[job.bank], 1)
            if valid(i, u, -1):
                job = side_job(i, u, "XT")
                act.wait_ge(side_full, job.count)
                act.copy(xn2T[:, (u - 1) % 2], side[:, job.bank, 0:D].rearrange("p (k t) -> p k t", k=KD))\
                   .then_inc(side_read[job.bank], 1)
            if valid(i, u, 1):
                exponentials(u + 1, n + 2, range(SPLITS[3], H))

        turns(act, BODY, TURNS, DRAIN, step)

    @block.gpsimd
    def _(pool):
        def pool_wait(signal, value):
            pool.wait_ge(signal, value)
            pool.tensor_tensor(waited_pool[:], eps[:, 0:1], eps[:, 0:1], ALU.add)

        pool.memset(kbd[:], 0.0)
        pool.memset(vbd[:], 0.0).then_inc(bd_zero, 1)
        pool.memset(minus_half[:], -0.5)
        pool.memset(eps[:], EPS)
        pool.memset(ones[:], 1.0)
        pool.memset(before[:, 1], 0.0)
        pool.memset(picked[:, 1], 0.0)
        pool.memset(rows[:, :, CW], 1.0)
        pool.memset(counts[:, 0:1], float(TILES))
        pool.memset(zeros[:], 0.0).then_inc(zeros_set, 1)
        pool.iota(rows[:, :, ID].bitcast(I32), pattern=[[P, BODY]], base=-TOK_PER_TURN, channel_multiplier=1)
        for t in range(2):
            pool.iota(first_row_i[:, t], pattern=[[ROOM, E]], base=ROOM + 1, channel_multiplier=0).then_inc(iota_set, 1)
        pool.iota(turn_i[:], pattern=[[0, 1]], base=TOK_PER_TURN, channel_multiplier=0).then_inc(iota_set, 1)
        pool.wait_ge(zeros_set, 1)
        pool.wait_ge(iota_set, 3)
        pool.tensor_copy(first_row[:], first_row_i[:])
        pool.affine_select(out=earlier[:], in_=ones[:], compare_op=ALU.is_gt, fill=0.0, base=0,
                           pattern=[[1, P]], channel_multiplier=-1)
        pool.memset(ident[:], 0.0).then_inc(ident_zero, 1)
        pool.wait_ge(ident_zero, 1)
        pool.affine_select(out=ident[:], in_=ident[:], compare_op=ALU.not_equal, fill=1.0, base=0,
                           pattern=[[-1, P]], channel_multiplier=1).then_inc(consts_set, 1)

        def reciprocal_deviation(slot, norms, steps):
            pool.wait_ge(stats_ready, steps)
            pool.tensor_tensor(veps[:, slot, norms], mv[:, slot, norms, 1], eps[:, norms], ALU.add).then_inc(veps_ready, 1)
            pool.wait_ge(veps_ready, steps)
            pool.tensor_tensor(rstd[:, slot, norms], veps[:, slot, norms], minus_half[:, norms], ALU.pow)\
                .then_inc(rstd_ready, 1)

        def residual(u, loads):
            pool.wait_ge(xres_in[u % 2], loads)
            pool.tensor_tensor(xres[:, u % 2], xres[:, u % 2], bo_b[:], ALU.add).then_inc(residual_ready, 1)

        for m in range(8):
            reciprocal_deviation(m % 2, slice(1, 2), m + 1)
        pool.wait_ge(consts_in, CONSTS)
        residual(0, 16)

        def step(i, u):
            n = i * BODY + u
            norms = slice(0 if valid(i, u, -1) else 1, 2 if valid(i, u, 8) else 1)
            if norms.start < norms.stop:
                reciprocal_deviation(u % 2, norms, n + 9)
            if valid(i, u, 1):
                residual(u + 1, i * (8 * BODY) + 16 * ((u + 1) // 2 + 1))
            if valid(i, u, -6):
                m, s, t = (u - 6) % BODY, (u - 6) // 2 % 2, u % 2
                if t == 0:
                    pool.wait_ge(slots_ready, i * (BODY // 2) + (u - 4) // 2)
                pool.tensor_tensor(rows[:, m, ID:ID + 1].bitcast(I32), rows[:, m, ID:ID + 1].bitcast(I32), turn_i[:], ALU.add)\
                    .then_inc(numbered, 1)
                pool_wait(numbered, i * BODY + (u - 5))
                for k in range(TOPK):
                    pool.indirect_dma_start(queue_d, bass.IndirectOffsetOnAxis(ap=slots[:, s, t, k:k + 1], axis=0),
                                            rows[:, m], None).then_inc(queued[m], 16)
            if u % 2 and valid(i, u, -5):
                s = (u - 5) // 2 % 2
                pool.wait_ge(routed, i * (BODY // 2) + (u - 3) // 2)
                if valid(i, u, -9):
                    unloaded(pool, side_job(i, u - 3, "PL"))
                pool.tensor_tensor(before[:, s, 0], before[:, 1 - s, 1], picked[:, 1 - s, 1], ALU.add).then_inc(before_step, 1)
                pool.wait_ge(before_step, i * BODY + (u - 4))
                pool.tensor_tensor(before[:, s, 1], before[:, s, 0], picked[:, s, 0], ALU.add).then_inc(before_step, 1)

        turns(pool, BODY, TURNS, DRAIN, step)
        pool.tensor_tensor(counts[:, 1:EA], before[:, 1, 1], picked[:, 1, 1], ALU.add).then_inc(counted, 1)
        for m in range(BODY):
            pool.wait_ge(queued[m], 16 * TOPK * TURNS)
        pool.wait_ge(counted, 1)

    @block.vector
    def _(dve):
        def wait_on_copy(sem, value, of):
            dve.wait_ge(sem, value)
            dve.tensor_copy(waited[:, 0:of.shape[1]], of)

        def first_stats(u, loads):
            dve.wait_ge(xin_in[u % 4], loads)
            return dve.bn_stats(bn[:, u % 2, 1], xin[:, u % 4])

        def normalise(to, of, slot, norm):
            return dve.tensor_scalar(to, of, mv[:, slot, norm, 0:1], rstd[:, slot, norm:norm + 1], ALU.subtract, ALU.mult)

        def maxima(u, tiles):
            dve.wait_ge(S_full, tiles)
            dve.tensor_reduce(rowmax[:, u % 2], S[:, u % 2].rearrange("p (h c) -> p h c", c=C), AX.X, ALU.max).then_inc(max_ready, 1)
            dve.wait_ge(max_ready, tiles)
            dve.tensor_scalar(rowneg[:, u % 2], rowmax[:, u % 2], -1.0, None, ALU.mult).then_inc(maxima_ready, 1)

        def divide(u, tiles):
            p = probs[:, u % 2].rearrange("p (h c) -> p h c", c=C)
            dve.wait_ge(exp_done, tiles)
            dve.reciprocal(rowinv[:, u % 2], rowsum[:, u % 2]).then_inc(inv_ready, 1)
            dve.wait_ge(inv_ready, tiles)
            dve.tensor_tensor(p, p, rowinv[:, u % 2].unsqueeze(2).to_broadcast([P, H, C]), ALU.mult)\
               .then_inc(probs_ready, 1)

        def split(name, s, job, at, i=0):
            unloaded(dve, job)
            dve.tensor_copy(prep_views(name, s, 0), staged[:, at % 4]).then_inc(split_high, 1)
            dve.wait_ge(split_high, i * PREP_PER_TURN + (at + 1))
            dve.tensor_tensor(prep_views(name, s, 1), staged[:, at % 4], prep_views(name, s, 0).bitcast(F32), ALU.subtract)\
               .then_inc(split_done, 1)

        for m in range(8):
            first_stats(m, 16 * (m // 4 + 1)).then_inc(bn_done, 1)
            dve.wait_ge(bn_done, m + 1)
            dve.bn_aggr(mv[:, m % 2, 1], bn[:, m % 2, 1]).then_inc(stats_ready, 1)
            dve.wait_ge(rstd_ready, m + 1)
            normalise(xn[:, m // TPB, m % TPB], xin[:, m % 4], m % 2, 1).then_inc(xn_ready, 1)
        for at, name in enumerate(PREP_ORDER):
            split(name, 0, prep_job(0, 0, name), at)
        dve.wait_ge(consts_in, CONSTS)
        maxima(0, 1)
        maxima(1, 2)
        divide(0, 1)

        def route_scores(i, u, c):
            s = (u - 5) // 2 % 2
            unloaded(dve, side_job(i, u - 2, "RT"))
            dve.tensor_scalar(denom[:], explog[:, s], 1.0, None, ALU.add).then_inc(scored, 1)
            dve.wait_ge(scored, c * 2 + 1)
            dve.reciprocal(score[:], denom[:]).then_inc(scored, 1)
            dve.wait_ge(scored, c * 2 + 2)
            dve.tensor_tensor(biased[:], score[:], gb_b[:], ALU.add).then_inc(biased_ready, 1)

        def route_best(c):
            wait_on_copy(biased_ready, c + 1, biased[:, 0:1, 0:1])
            for t in range(2):
                top = dve.max(top8[:, t], biased[:, t])
            top.then_inc(top_ready, 1)
            dve.wait_ge(top_ready, c * 2 + 1)
            dve.memset(top8[:, :, TOPK:8], NEVER).then_inc(top_ready, 1)

        def route_picks(u, c):
            s = (u - 5) // 2 % 2
            wait_on_copy(top_ready, c * 2 + 2, top8[:, 0:1, 0:1])
            for t in range(2):
                top = dve.match_replace(rest[:, t], top8[:, t], biased[:, t], -NEVER)
            top.then_inc(picked_ready, 1)
            dve.wait_ge(picked_ready, c * 2 + 1)
            dve.tensor_tensor(picked[:, s], rest[:], biased[:], ALU.not_equal).then_inc(picked_ready, 1)

        def route_weights(u, c):
            s = (u - 5) // 2 % 2
            dve.wait_ge(picked_ready, c * 2 + 2)
            dve.tensor_tensor(weight[:], picked[:, s], score[:], ALU.mult).then_inc(weight_ready, 1)
            dve.wait_ge(weight_ready, c + 1)
            dve.tensor_reduce(wsum[:], weight[:], AX.X, ALU.add).then_inc(wsum_ready, 1)
            dve.wait_ge(wsum_ready, c * 2 + 1)
            dve.reciprocal(winv[:], wsum[:]).then_inc(wsum_ready, 1)
            dve.wait_ge(wsum_ready, c * 2 + 2)
            m = (u - 5) % BODY
            dve.scalar_tensor_tensor(out=rows[:, m:m + 2, CW + 1:ROW], in0=weight[:], scalar=ROUTE_SCALE,
                                     in1=winv[:].unsqueeze(2).to_broadcast([P, 2, E]), op0=ALU.mult, op1=ALU.mult)\
               .then_inc(routed, 1)

        def queue_slots(i, u, c):
            s = (u - 6) // 2 % 2
            job = side_job(i, u, "PL")
            dve.wait_ge(side_full, job.count)
            dve.tensor_tensor(place[:], side[:, job.bank, 0:2 * E].rearrange("p (t e) -> p t e", t=2), first_row[:],
                              ALU.add).then_inc(side_read[job.bank], 1)
            unloaded(dve, job)
            dve.tensor_tensor(placed[:], place[:], picked[:, s], ALU.mult).then_inc(place_step, 1)
            wait_on_copy(place_step, c * 2 + 1, placed[:, 0:1, 0:1])
            for t in range(2):
                top = dve.max(place8[:, t], placed[:, t])
            top.then_inc(place_step, 1)
            dve.wait_ge(place_step, c * 2 + 2)
            if valid(i, u, -9):
                dve.wait_ge(queued[(u - 9) % BODY], i * (16 * TOPK) + 16 * TOPK * ((u - 9) // BODY + 1))
            if valid(i, u, -10):
                dve.wait_ge(queued[(u - 10) % BODY], i * (16 * TOPK) + 16 * TOPK * ((u - 10) // BODY + 1))
            dve.tensor_scalar(slots[:, s], place8[:, :, 0:TOPK], -1.0, None, ALU.add).then_inc(slots_ready, 1)

        def step(i, u):
            n = i * BODY + u
            second, first = valid(i, u, -1), valid(i, u, 8)
            routes, c = u % 2 == 1 and valid(i, u, -5), i * (BODY // 2) + (u - 5) // 2
            norms = slice(0 if second else 1, 2 if first else 1)
            if second:
                job = side_job(i, u - 1, "O")
                s = (u - 1) % 2
                dve.wait_ge(side_full, job.count)
                dve.wait_ge(residual_ready, n)
                if valid(i, u, -3):
                    dve.wait_ge(x1_stored[s], i * (8 * BODY) + 16 * ((u - 1) // 2))
                dve.tensor_tensor(x1[:, s], side[:, job.bank, 0:D], xres[:, s], ALU.add).then_inc(side_read[job.bank], 1)
                unloaded(dve, job)
                last = dve.bn_stats(bn[:, u % 2, 0], x1[:, s])
            if first:
                last = first_stats(u, i * 32 + 16 * (u // 4 + 3))
            if second or first:
                last.then_inc(bn_done, 1)
                wait_on_copy(bn_done, n + 9, bn[:, u % 2, norms, 0:1])
                if second:
                    last = dve.bn_aggr(mv[:, u % 2, 0], bn[:, u % 2, 0])
                if first:
                    last = dve.bn_aggr(mv[:, u % 2, 1], bn[:, u % 2, 1])
                last.then_inc(stats_ready, 1)
            if routes:
                route_scores(i, u, c)
            if valid(i, u, 0):
                for half in range(2):
                    pairs = slice(half * PAIRS // 2, (half + 1) * PAIRS // 2)
                    dve.wait_ge(probsT_high, n * 2 + (half + 1))
                    dve.tensor_tensor(probsT_hl[:, u % 2, 1, pairs], PT[:, pairs], probsT_hl[:, u % 2, 0, pairs].bitcast(F32),
                                      ALU.subtract).then_inc(probsT_low, 1)
            if second or first:
                dve.wait_ge(rstd_ready, n + 9)
            if second:
                if valid(i, u, -9):
                    dve.wait_ge(queued[(u - 1) % BODY], i * (16 * TOPK) + 16 * TOPK * ((u - 9) // BODY + 1))
                    dve.wait_ge(shared_queued[(u - 1) % BODY], i * 16 + 16 * ((u - 9) // BODY + 1))
                normalise(rows[:, (u - 1) % BODY, 0:D], x1[:, (u - 1) % 2], u % 2, 0).then_inc(xn2_ready, 1)
            if first:
                normalise(xn[:, u // TPB % 2, u % TPB], xin[:, u % 4], u % 2, 1).then_inc(xn_ready, 1)
            names = QUARTER[u % TPB] if prepares(i, u) else []

            def splits(jobs):
                for name in jobs:
                    split(name, (u // TPB + 1) % 2, side_job(i, u, name), prep_at(u, name), i)

            if routes:
                route_best(c)
            if valid(i, u, 2):
                maxima(u + 2, n + 3)
            if routes:
                route_picks(u, c)
            splits(names[:1])
            if routes:
                route_weights(u, c)
            splits(names[1:2])
            if u % 2 == 0 and valid(i, u, -6):
                queue_slots(i, u, i * (BODY // 2) + (u - 6) // 2)
            if valid(i, u, 1):
                divide(u + 1, n + 2)
            splits(names[2:])

        turns(dve, BODY, TURNS, DRAIN, step)


E_TURNS = STEPS // E_BODY
SHARED = TOK // STEP // E_BODY
PER_SHARED = E // SHARED


def e_turns(eng, drain, step):
    for u in range(E_BODY):
        step(0, u, True)
    with eng.Fori(1, SHARED) as i:
        for u in range(E_BODY):
            step(i, u, True)
    with eng.Fori(SHARED, E_TURNS - 1) as i:
        for u in range(E_BODY):
            step(i, u, False)
    for u in range(E_BODY):
        step(E_TURNS - 1, u, False)
    for u in range(drain):
        step(E_TURNS, u, False)


HALVES = STEP // P


def phase_e(nc, ctx, w13, w2, w13_s, w2_s, ident, ones, counts, scratch, out_sums):
    queue_d, table_d, ends_d = (scratch[k] for k in ("queue", "table", "ends"))
    CHUNKS = 2

    def sb(name, shape, dt=F32):
        return ctx.enter_context(nc.sbuf_tensor(name, shape, dt))

    def sem(name):
        return ctx.enter_context(nc.semaphore(name))

    w13_hl = sb("w13_hl", [P, EA, KD, 2, 2 * I], F32R)
    w2_hl = sb("w2_hl", [P, EA, 2, D], F32R)
    stage = sb("stage", [P, 2, 3, D])
    steps_t = sb("steps_t", [1, 6 * P], I32)
    X = sb("X", [P, E_BODY, HALVES, ROW])
    xT_hl = sb("xT_hl", [P, 2, 2, KD, STEP], F32R)
    gated = sb("gated", [P, 2, HALVES, I])
    hid = sb("hid", [P, 2, HALVES, I])
    hidT_hl = sb("hidT_hl", [P, 2, 2, STEP], F32R)
    y = sb("y", [P, 4, HALVES, D])
    upto = sb("upto", [EA, 2, EA])
    number = sb("number", [P, CHUNKS])
    number_i = sb("number_i", [P, CHUNKS], I32)
    base = sb("base", [EA, 1])
    base_i = sb("base_i", [EA, 1], I32)
    padding = sb("padding", [P, HALVES, ROW])
    n_s = sb("n_s", [EA, P])
    guess = sb("guess", [EA, P])
    guess_i = sb("guess_i", [EA, P], I32)
    guessed = sb("guessed", [EA, P])
    short = sb("short", [EA, P])
    blocks = sb("blocks", [EA, P])
    cum = sb("cum", [P, 2, EA])
    gone = sb("gone", [P, 2, CHUNKS, EA])
    sums = sb("gone_sums", [P, 2, CHUNKS])
    within = sb("within", [P, CHUNKS])
    used = sb("used", [P, CHUNKS])
    offset = sb("offset", [P, CHUNKS])
    masked = sb("masked", [P, CHUNKS])
    table = sb("table", [P, 3, CHUNKS], I32)
    waits = sb("waits", [P, CHUNKS])
    waits_i = sb("waits_i", [P, CHUNKS], I32)
    opening = sb("opening", [P, CHUNKS])
    ends_i = sb("ends_i", [EA, 1], I32)
    ends_row = sb("ends_row", [1, EA], I32)
    waited_e = sb("waited_e", [P, 2])
    XT = ctx.enter_context(nc.psum_tensor("XT", [P, 2, KD, STEP], F32))
    UP = ctx.enter_context(nc.psum_tensor("UP", [P, 2, HALVES, 2 * I], F32))
    HT = ctx.enter_context(nc.psum_tensor("HT", [P, 2, 2 * STEP], F32))
    Y = ctx.enter_context(nc.psum_tensor("Y", [P, 2, HALVES, D], F32))

    N_PS, CUM = HT[0:EA, 1, STEP:STEP + P], HT[:, 1, STEP + P:STEP + P + 2 * EA]

    steps_in = sem("steps_in")
    numbers_set = sem("numbers_set")
    t_consts = sem("t_consts")
    n_full = sem("n_full")
    made = sem("made")
    blocks_ready = sem("blocks_ready")
    cum_full = sem("cum_full")
    table_ready = sem("table_ready")
    ends_ready = sem("ends_ready")
    table_stored = sem("table_stored")
    ends_stored = sem("ends_stored")
    ends_in = sem("ends_in")
    padded = sem("padded")
    stage_in = [sem("stage_in0"), sem("stage_in1")]
    w_high = sem("w_high")
    w_low = sem("w_low")
    waited_set = sem("waited_set")
    may_add = sem("may_add")
    rows_in = [sem(f"rows_in{i}") for i in range(E_BODY)]
    xt_full = sem("xt_full")
    x_high = sem("x_high")
    x_low = sem("x_low")
    up_full = sem("up_full")
    gated_ready = sem("gated_ready")
    hid_ready = sem("hid_ready")
    ht_full = sem("ht_full")
    ht_high = sem("ht_high")
    ht_low = sem("ht_low")
    y_full = sem("y_full")
    y_ready = sem("y_ready")
    added = [sem("added0"), sem("added1")]
    block = ctx.enter_context(nc.Block())

    def ok(i, u, d):
        return 0 <= i * E_BODY + u + d < STEPS if isinstance(i, int) else True

    def loads(i, u):
        return i * 16 + 16 * (u // E_BODY + 1)

    def adds(i, u):
        return i * (16 * E_BODY) + 32 * (u // 2 + 1)

    def first_row(i, u):
        m = i * E_BODY + u
        return steps_t[0:1, bass.ds(m, 1)]

    def expert(i, u):
        m = i * E_BODY + (2 * P + u)
        return steps_t[0:1, bass.ds(m, 1)]

    def order(i, u):
        m = i * E_BODY + (4 * P + u)
        return steps_t[0:1, bass.ds(m, 1)]

    def staged(i, u):
        q = u * PER_SHARED // E_BODY + 1
        return i * PER_SHARED + q, q % 2, i * (16 * PER_SHARED) + 32 * (q // 2 + 1)

    def splits(u):
        return u * PER_SHARED % E_BODY == 0

    @block.sync
    def _(sp):
        def load_weights(s, a, b):
            sp.dma_start(stage[:, s, 0:KD], a).then_inc(stage_in[s], 16)
            sp.dma_start(stage[:, s, KD], b).then_inc(stage_in[s], 16)

        def load_rows(i, u, row):
            if ok(i, u, -E_BODY):
                sp.wait_ge(added[u % 2], adds(i, u - E_BODY))
            sp.dma_start(X[:, u], queue_d[bass.ds(row, STEP)].rearrange("(t p) d -> p t d", p=P))\
                .then_inc(rows_in[u], 16)

        def step(i, u, shared):
            if shared:
                load_rows(i, u, i * (E_BODY * STEP) + u * STEP)
                if splits(u):
                    q, s, _ = staged(i, u)
                    if ok(i, u, -1):
                        sp.wait_ge(w_low, i * (2 * PER_SHARED) + 2 * (u * PER_SHARED // E_BODY))
                    a, b = w13_q(q), w2_q(q)
                    load_weights(s, a, b)
            else:
                load_rows(i, u, sp.value_load(first_row(i, u), min_val=0, max_val=EA * ROOM))

        def w13_q(q):
            return w13[:, bass.ds(q - 1, 1)].rearrange("(k p) a n -> p k (a n)", p=P)

        def w2_q(q):
            return w2[:, bass.ds(q - 1, 1)].rearrange("p a n -> p (a n)")

        load_weights(0, w13_s.rearrange("(k p) n -> p k n", p=P), w2_s)
        for u in range(E_BODY):
            step(0, u, True)
        sp.wait_ge(ends_ready, 1)
        sp.dma_start(ends_d, ends_i[:]).then_inc(ends_stored, 16)
        sp.wait_ge(ends_stored, 16)
        sp.dma_start(ends_row[:], ends_d.rearrange("e a -> a e", a=1)).then_inc(ends_in, 16)
        sp.dma_start(queue_d[EA * ROOM:].rearrange("(t p) d -> p t d", p=P), padding[:]).then_inc(padded, 16)
        sp.wait_ge(table_ready, 1)
        for a in range(3):
            sp.dma_start(table_d[a].rearrange("(p c) -> p c", c=CHUNKS), table[:, a]).then_inc(table_stored, 16)
        sp.wait_ge(table_stored, 48)
        sp.dma_start(steps_t[:], table_d.rearrange("a n -> (a n)").rearrange("(o n) -> o n", o=1)).then_inc(steps_in, 16)
        sp.wait_ge(ends_in, 16)
        with sp.Fori(1, E // E_BODY + 1) as i:
            for u in range(E_BODY):
                step(i, u, True)
                e = i * E_BODY + (u - E_BODY + 1)
                end = sp.value_load(ends_row[0:1, bass.ds(e, 1)], min_val=0, max_val=EA * ROOM)
                sp.dma_start(queue_d[bass.ds(end, STEP)].rearrange("(t p) d -> p t d", p=P), padding[:]).then_inc(padded, 16)
        for i in range(E // E_BODY + 1, SHARED):
            for u in range(E_BODY):
                step(i, u, True)
        sp.wait_ge(padded, 16 * EA)
        sp.wait_ge(steps_in, 16)
        with sp.Fori(SHARED, E_TURNS) as i:
            for u in range(E_BODY):
                step(i, u, False)

    @block.tensor
    def _(pe):
        pe.matmul(N_PS, counts[:], ones[:], start=True, stop=True).then_inc(n_full, 1)
        pe.wait_ge(t_consts, 1)
        pe.wait_ge(blocks_ready, 1)
        pe.matmul(CUM, blocks[:], upto[:].rearrange("p a e -> p (a e)"), start=True, stop=True).then_inc(cum_full, 1)

        def transposes(i, u):
            m = i * E_BODY + u
            if ok(i, u, -2):
                pe.wait_ge(x_low, m - 1)
            pe.wait_ge(rows_in[u % E_BODY], loads(i, u))
            for k in range(KD):
                for t in range(HALVES):
                    mm = pe.transpose(XT[:, u % 2, k, t * P:t * P + P], X[:, u % E_BODY, t, k * P:k * P + P], ident[:])
            mm.then_inc(xt_full, 1)

        transposes(0, 0)
        transposes(0, 1)
        pe.wait_ge(w_low, 2)

        def step(i, u, shared):
            m = i * E_BODY + u
            if not shared and u == 0:
                pe.wait_ge(steps_in, 16)
                pe.wait_ge(w_low, 2 * EA)
            if ok(i, u, 0):
                e = 0 if shared else pe.value_load(expert(i, u), min_val=0, max_val=EA - 1)
                if ok(i, u, -2):
                    pe.wait_ge(hid_ready, m - 1)
                pe.wait_ge(x_low, m + 1)
                passes = [(xh, wh, k) for xh, wh in ((0, 0), (0, 1), (1, 0)) for k in range(KD)]
                for t in range(HALVES):
                    for xh, wh, k in passes:
                        mm = pe.matmul(UP[:, u % 2, t], xT_hl[:, u % 2, xh, k, t * P:t * P + P],
                                       w13_hl[:, bass.ds(e, 1), k, wh, :].rearrange("p a n -> p (a n)"),
                                       start=((xh, wh, k) == passes[0]), stop=((xh, wh, k) == passes[-1]))
                mm.then_inc(up_full, 1)
            if ok(i, u, 2):
                transposes(i, u + 2)
            if ok(i, u, -1):
                if ok(i, u, -3):
                    pe.wait_ge(ht_low, m - 2)
                pe.wait_ge(hid_ready, m)
                for t in range(HALVES):
                    mm = pe.transpose(HT[:, (u - 1) % 2, t * P:t * P + P], hid[:, (u - 1) % 2, t], ident[:])
                mm.then_inc(ht_full, 1)
            if ok(i, u, -2):
                e = 0 if shared else pe.value_load(expert(i, u - 2), min_val=0, max_val=EA - 1)
                if ok(i, u, -4):
                    pe.wait_ge(y_ready, m - 3)
                pe.wait_ge(ht_low, m - 1)
                for t in range(HALVES):
                    for hh, wh in ((0, 0), (0, 1), (1, 0)):
                        mm = pe.matmul(Y[:, u % 2, t], hidT_hl[:, u % 2, hh, t * P:t * P + P],
                                       w2_hl[:, bass.ds(e, 1), wh, :].rearrange("p a d -> p (a d)"),
                                       start=(hh + wh == 0), stop=(hh == 1))
                mm.then_inc(y_full, 1)

        e_turns(pe, 3, step)

    @block.scalar
    def _(act):
        def high_weights(q, s, loads):
            act.wait_ge(stage_in[s], loads)
            act.copy(w13_hl[:, bass.ds(q, 1), :, 0], stage[:, s:s + 1, 0:KD]).then_inc(w_high, 1)
            act.copy(w2_hl[:, bass.ds(q, 1), 0], stage[:, s:s + 1, KD]).then_inc(w_high, 1)

        high_weights(0, 0, 32)

        def x_highs(i, u):
            m = i * E_BODY + u
            act.wait_ge(xt_full, m + 1)
            if ok(i, u, -2):
                act.wait_ge(up_full, m - 1)
            act.copy(xT_hl[:, u % 2, 0], XT[:, u % 2]).then_inc(x_high, 1)

        x_highs(0, 0)
        x_highs(0, 1)

        def step(i, u, shared):
            m = i * E_BODY + u
            if ok(i, u, 0):
                act.wait_ge(up_full, m + 1)
                if ok(i, u, -2):
                    act.wait_ge(hid_ready, m - 1)
                act.activation(gated[:, u % 2], UP[:, u % 2, :, 0:I], ACT.Silu).then_inc(gated_ready, 1)
            if ok(i, u, 2):
                x_highs(i, u + 2)
            if ok(i, u, -1):
                act.wait_ge(ht_full, m)
                if ok(i, u, -3):
                    act.wait_ge(y_full, m - 2)
                act.copy(hidT_hl[:, (u - 1) % 2, 0], HT[:, (u - 1) % 2, 0:STEP]).then_inc(ht_high, 1)
            if ok(i, u, -2):
                act.wait_ge(y_full, m - 1)
                if ok(i, u, -6):
                    act.wait_ge(added[u % 2], adds(i, u - 6))
                act.copy(y[:, (u - 2) % 4], Y[:, u % 2]).then_inc(y_ready, 1)
            if shared and splits(u):
                high_weights(*staged(i, u))

        e_turns(act, 3, step)

    @block.vector
    def _(dve):
        steps = [0]

        def then(instruction):
            steps[0] += 1
            instruction.then_inc(made, 1)
            dve.wait_ge(made, steps[0])

        dve.wait_ge(t_consts, 1)
        dve.wait_ge(n_full, 1)
        then(dve.tensor_copy(n_s[:], N_PS))
        dve.tensor_tensor(ends_i[:], n_s[:, 0:1], base[:], ALU.add).then_inc(ends_ready, 1)
        then(dve.tensor_scalar(guess[:], n_s[:], 1.0 / STEP, 0.5 - 0.5 / STEP, ALU.mult, ALU.add))
        then(dve.tensor_copy(guess_i[:], guess[:]))
        then(dve.tensor_copy(guessed[:], guess_i[:]))
        then(dve.scalar_tensor_tensor(out=short[:], in0=guessed[:], scalar=float(STEP), in1=n_s[:], op0=ALU.mult, op1=ALU.is_lt))
        dve.tensor_tensor(blocks[:], guessed[:], short[:], ALU.add).then_inc(blocks_ready, 1)

        def low_weights(q, s, highs):
            dve.wait_ge(w_high, highs)
            dve.tensor_tensor(w13_hl[:, bass.ds(q, 1), :, 1], stage[:, s:s + 1, 0:KD], w13_hl[:, bass.ds(q, 1), :, 0].bitcast(F32),
                              ALU.subtract).then_inc(w_low, 1)
            dve.tensor_tensor(w2_hl[:, bass.ds(q, 1), 1], stage[:, s:s + 1, KD], w2_hl[:, bass.ds(q, 1), 0].bitcast(F32),
                              ALU.subtract).then_inc(w_low, 1)

        low_weights(0, 0, 2)

        def x_lows(i, u):
            m = i * E_BODY + u
            dve.wait_ge(x_high, m + 1)
            dve.tensor_tensor(xT_hl[:, u % 2, 1], XT[:, u % 2], xT_hl[:, u % 2, 0].bitcast(F32), ALU.subtract).then_inc(x_low, 1)

        x_lows(0, 0)
        x_lows(0, 1)
        dve.wait_ge(cum_full, 1)
        then(dve.tensor_copy(cum[:], CUM.rearrange("p (a e) -> p a e", a=2)))
        for c in range(CHUNKS):
            last = dve.tensor_scalar(gone[:, 0, c], cum[:, 0], number[:, c:c + 1], None, ALU.is_le)
        then(last)
        then(dve.tensor_tensor(gone[:, 1], gone[:, 0], cum[:, 1:2].to_broadcast([P, CHUNKS, EA]), ALU.mult))
        then(dve.tensor_reduce(sums[:], gone[:], AX.X, ALU.add))
        dve.tensor_scalar(used[:], sums[:, 0], EA - 0.5, None, ALU.is_lt)
        dve.tensor_scalar(offset[:], sums[:, 0], float(ROOM), None, ALU.mult)
        then(dve.tensor_tensor(within[:], number[:], sums[:, 1], ALU.subtract))
        then(dve.scalar_tensor_tensor(out=masked[:], in0=within[:], scalar=float(STEP), in1=used[:], op0=ALU.mult, op1=ALU.mult))
        then(dve.tensor_scalar(opening[:], masked[:], 0.0, None, ALU.is_equal))
        dve.scalar_tensor_tensor(out=table[:, 2], in0=opening[:], scalar=32.0, in1=waits[:], op0=ALU.mult, op1=ALU.add)
        dve.tensor_tensor(table[:, 0], masked[:], offset[:], ALU.add)
        dve.tensor_scalar(table[:, 1], sums[:, 0], float(EA - 1), None, ALU.min).then_inc(table_ready, 1)


        def step(i, u, shared):
            m = i * E_BODY + u
            if not shared and u == 0:
                dve.wait_ge(steps_in, 16)
            if ok(i, u, 0):
                e = 0 if shared else dve.value_load(expert(i, u), min_val=0, max_val=EA - 1)
                if ok(i, u, -2):
                    dve.wait_ge(ht_full, m - 1)
                dve.wait_ge(gated_ready, m + 1)
                for t in range(HALVES):
                    last = dve.scalar_tensor_tensor(out=hid[:, u % 2, t], in0=UP[:, u % 2, t, I:2 * I],
                                                    scalar=X[:, u % E_BODY, t, bass.ds(e + CW, 1)],
                                                    in1=gated[:, u % 2, t], op0=ALU.mult, op1=ALU.mult)
                last.then_inc(hid_ready, 1)
            if ok(i, u, 2):
                x_lows(i, u + 2)
            if ok(i, u, -1):
                dve.wait_ge(ht_high, m)
                dve.tensor_tensor(hidT_hl[:, (u - 1) % 2, 1], HT[:, (u - 1) % 2, 0:STEP],
                                  hidT_hl[:, (u - 1) % 2, 0].bitcast(F32), ALU.subtract).then_inc(ht_low, 1)
            if shared and splits(u):
                q, s, _ = staged(i, u)
                low_weights(q, s, i * (2 * PER_SHARED) + 2 * (u * PER_SHARED // E_BODY + 2))

        e_turns(dve, 3, step)

    @block.gpsimd
    def _(pool):
        pool.iota(number_i[:], pattern=[[1, CHUNKS]], base=0, channel_multiplier=CHUNKS).then_inc(numbers_set, 1)
        pool.iota(waits_i[:], pattern=[[32, CHUNKS]], base=-32, channel_multiplier=32).then_inc(numbers_set, 1)
        pool.iota(base_i[:], pattern=[[0, 1]], base=0, channel_multiplier=ROOM).then_inc(numbers_set, 1)
        pool.memset(padding[:], 0.0).then_inc(numbers_set, 1)
        pool.wait_ge(numbers_set, 4)
        pool.tensor_copy(waits[:], waits_i[:])
        pool.tensor_copy(number[:], number_i[:])
        pool.tensor_copy(base[:], base_i[:])
        pool.tensor_copy(upto[:, 1], ident[0:EA, 0:EA])
        pool.affine_select(out=upto[:, 0], in_=ones[0:EA, 0:EA], compare_op=ALU.is_ge, fill=0.0, base=0,
                           pattern=[[1, EA]], channel_multiplier=-1)
        pool.iota(padding[:, :, ID].bitcast(I32), pattern=[[P, STEP // P]], base=TOK, channel_multiplier=1)\
            .then_inc(t_consts, 1)
        def pool_wait(signal, value):
            pool.wait_ge(signal, value)
            pool.tensor_tensor(waited_pool[:], eps[:, 0:1], eps[:, 0:1], ALU.add)

        pool.memset(waited_e[:], 0.0).then_inc(waited_set, 1)
        pool.wait_ge(waited_set, 1)

        def step(i, u, shared):
            m = i * E_BODY + u
            if not shared and u == 0:
                pool.wait_ge(steps_in, 16)
            pool.wait_ge(y_ready, m + 1)
            if not shared:
                before = pool.value_load(order(i, u), min_val=32, max_val=16 * STEPS + 32)
                pool.wait_ge(added[(u - 1) % 2], before)
            if ok(i, u, -2):
                pool.wait_ge(added[u % 2], adds(i, u - 2))
            if ok(i, u, -1):
                pool.wait_ge(may_add, m)
            pool.tensor_tensor(waited_e[:, 0:1], waited_e[:, 1:2], waited_e[:, 1:2], ALU.add).then_inc(may_add, 1)
            for t in range(HALVES):
                pool.indirect_dma_start(out_sums, bass.IndirectOffsetOnAxis(ap=X[:, u % E_BODY, t, ID:ID + 1].bitcast(U32), axis=0),
                                        y[:, u % 4, t], None, compute_op=ALU.add).then_inc(added[u % 2], 16)

        e_turns(pool, 0, step)
        for s in range(2):
            pool.wait_ge(added[s], 16 * STEPS)


def kernel(**inputs):
    import numpy as np
    import concourse.bacc as bacc
    from concourse.bass_utils import run_bass_kernel_spmd

    a = {k: np.asarray(v) for k, v in inputs.items()}
    arrays = {
        "x": a["x"],
        "ctxT": a["ctx_1024"].reshape(B * C, D).T,
        "wq": a["L0_xattn_Wq"].T,
        "wk": a["L0_xattn_Wk"],
        "wv": a["L0_xattn_Wv"],
        "wo": a["L0_xattn_Wo"],
        "bo": a["L0_xattn_bo"],
        "gateT": a["L0_ffn_gate_w"].T,
        "gate_b": a["L0_ffn_gate_b"],
        "w13": a["L0_ffn_w13"].transpose(2, 0, 1),
        "w2": a["L0_ffn_w2"].transpose(2, 0, 1),
        "w13_s": a["L0_ffn_w13_s"].T,
        "w2_s": a["L0_ffn_w2_s"].T,
    }
    nc = bacc.Bacc("TRN2", target_bir_lowering=False, num_devices=1)
    feeds, args = {}, {}
    for name, value in arrays.items():
        value = np.ascontiguousarray(value)
        feeds[f"in_{name}"] = value
        args[name] = nc.dram_tensor(f"in_{name}", value.shape, mybir.dt.from_np(value.dtype), kind="ExternalInput").ap()
    args["sums"] = nc.dram_tensor("out_y", (SUMS, D), F32, kind="ExternalOutput").ap()
    build(nc, **args)
    r = run_bass_kernel_spmd(nc, [feeds], core_ids=[0])
    return np.asarray(r.results[0]["out_y"])[:TOK].reshape(B, N, D)
```
